# Optimizing a Trainium2 kernel written in Bass

```python
import numpy as np
import jax
import jax.numpy as jnp

def _softmax(x, axis=-1):
    return jax.nn.softmax(x, axis=axis)

def _gelu(x):
    return jax.nn.gelu(x, approximate=True)

def _silu(x):
    return jax.nn.silu(x)

def _sigmoid(x):
    return jax.nn.sigmoid(x)

def _layernorm(x, axis=-1, eps=1e-05):
    m = jnp.mean(x, axis=axis, keepdims=True)
    v = jnp.var(x, axis=axis, keepdims=True)
    return (x - m) / jnp.sqrt(v + eps)

def _scatter_add(tgt, idx, src, axis=0):
    return tgt.at[idx].add(src)

def _segment_sum(src, seg, n):
    return jax.ops.segment_sum(src, seg, n)
kernel_name = 'mk_prb_d1_jaxref_r8_664e59'

def setup_inputs(seed: int=0):
    np.random.seed(seed)
    _w = jnp.asarray

    def _L0_attn_setup():
        import jax, jax.numpy as jnp
        import numpy as np
        ALPHA = 0.99
        EMBED_DIM = 128
        SEQ_LEN = 256
        BATCH = 4
        key = jax.random.key(seed)
        k1, k2, k3 = jax.random.split(key, 3)
        x = jax.random.normal(k1, (BATCH, SEQ_LEN, EMBED_DIM), dtype=jnp.float32)
        scale = 1.0 / np.sqrt(EMBED_DIM)
        W_qkv = jax.random.uniform(k2, (3 * EMBED_DIM, EMBED_DIM), dtype=jnp.float32, minval=-scale, maxval=scale)
        b_qkv = jax.random.uniform(k3, (3 * EMBED_DIM,), dtype=jnp.float32, minval=-scale, maxval=scale)
        return {'x': x, 'W_qkv': W_qkv, 'b_qkv': b_qkv}
    _L0_attn_in = _L0_attn_setup()

    def _L0_ffn_setup():
        import jax, jax.numpy as jnp
        import numpy as np
        B, K, D = (128, 32, 128)
        E = 32
        H = int(D * 0.25)

        def _rsqrt_uniform(key, shape, d):
            bound = d ** (-0.5)
            return jax.random.uniform(key, shape, jnp.float32, -bound, bound)
        key = jax.random.key(seed)
        ks = jax.random.split(key, 7)
        return {'x': jax.random.normal(ks[0], (B, K, D), jnp.float32), 'router_w': _rsqrt_uniform(ks[1], (E, D), D), 'router_b': _rsqrt_uniform(ks[2], (E,), D), 'weights1': _rsqrt_uniform(ks[3], (E, D, H), H), 'bias1': _rsqrt_uniform(ks[4], (E, H), H), 'weights2': _rsqrt_uniform(ks[5], (E, H, D), D), 'bias2': _rsqrt_uniform(ks[6], (E, D), D)}
    _L0_ffn_in = _L0_ffn_setup()
    _d = {'L0_attn_x': _L0_attn_in['x'], 'L0_attn_W_qkv': _L0_attn_in['W_qkv'], 'L0_attn_b_qkv': _L0_attn_in['b_qkv'], 'L0_ffn_router_w': _L0_ffn_in['router_w'], 'L0_ffn_router_b': _L0_ffn_in['router_b'], 'L0_ffn_weights1': _L0_ffn_in['weights1'], 'L0_ffn_bias1': _L0_ffn_in['bias1'], 'L0_ffn_weights2': _L0_ffn_in['weights2'], 'L0_ffn_bias2': _L0_ffn_in['bias2']}
    _x0 = _d['L0_attn_x']
    _d['L0_attn_x'] = jax.random.normal(jax.random.fold_in(jax.random.key(seed), 1), (8, 256, 128), dtype=_x0.dtype)
    del _x0
    return _d

def reference(L0_attn_x, L0_attn_W_qkv, L0_attn_b_qkv, L0_ffn_router_w, L0_ffn_router_b, L0_ffn_weights1, L0_ffn_bias1, L0_ffn_weights2, L0_ffn_bias2):

    def _L0_attn_ref(x, W_qkv, b_qkv):
        import jax, jax.numpy as jnp
        import numpy as np
        ALPHA = 0.99
        EMBED_DIM = 128
        SEQ_LEN = 256
        BATCH = 4
        bs, sl, d = x.shape
        qkv = x @ W_qkv.T + b_qkv
        q, k, v = jnp.split(qkv, 3, axis=-1)
        idx = jnp.arange(sl)
        diff = (idx[:, None] - idx[None, :]).astype(jnp.float32)
        M = jnp.where(idx[:, None] >= idx[None, :], ALPHA ** diff, 0.0)
        dim_sqrt = jnp.float32(np.sqrt(d))
        scores = jnp.einsum('bqd,bkd->bqk', q, k) / dim_sqrt * M
        out = scores @ v
        return out

    def _L0_ffn_ref(x, router_w, router_b, weights1, bias1, weights2, bias2):
        import jax, jax.numpy as jnp
        import numpy as np
        B, K, D = (128, 32, 128)
        E = 32
        H = int(D * 0.25)

        def _rsqrt_uniform(key, shape, d):
            bound = d ** (-0.5)
            return jax.random.uniform(key, shape, jnp.float32, -bound, bound)
        b, k, d = x.shape
        x_flat = x.reshape(-1, d)
        n = x_flat.shape[0]
        logits = x_flat @ router_w.T + router_b
        routed_idx = jnp.argmax(logits, axis=-1)

        def expert_mlp(w1, b1, w2, b2):
            h = jax.nn.relu(x_flat @ w1 + b1)
            return jax.nn.relu(h @ w2 + b2)
        y_all = jax.vmap(expert_mlp)(weights1, bias1, weights2, bias2)
        out_flat = y_all[routed_idx, jnp.arange(n)]
        return out_flat.reshape(b, k, d)
    x = L0_attn_x
    xn = _layernorm(x, axis=-1)
    x = x + _L0_attn_ref(xn, L0_attn_W_qkv, L0_attn_b_qkv) + _L0_ffn_ref(xn, L0_ffn_router_w, L0_ffn_router_b, L0_ffn_weights1, L0_ffn_bias1, L0_ffn_weights2, L0_ffn_bias2)
    return x

_drawn_inputs = setup_inputs


def setup_inputs(seed=0):
    import zlib

    import numpy as np

    out = dict(_drawn_inputs(seed))
    spreads = {}
    factors = {'L0_ffn_bias1': 8.0, 'L0_ffn_bias2': 3.534}
    for name, (base, spread) in spreads.items():
        noise = np.random.default_rng([zlib.crc32(name.encode()), seed]).standard_normal(out[name].shape)
        drawn = base * np.exp(spread * noise) if base else spread * noise
        out[name] = jnp.asarray(drawn.astype(out[name].dtype))
    for name, factor in factors.items():
        out[name] = (out[name] * factor).astype(out[name].dtype)
    return out
```

```python
from contextlib import ExitStack

import numpy as np

import concourse.bass as bass
from concourse import mybir

F32 = mybir.dt.float32
F32R = mybir.dt.float32r
BF16 = mybir.dt.bfloat16
ALU = mybir.AluOpType
ACT = mybir.ActivationFunctionType
AX = mybir.AxisListType

P = 128
D = 128
SEQ = 256
BATCH = 8
TOK = BATCH * SEQ
GT = 512
NG = TOK // GT
NT = GT // P
NS = GT // SEQ
E = 32
H = 32
EB = P // H
NB = E // EB
VW = D + E + 1
ALPHA = 0.99
EPS = 1e-5
BIG = 2.0 ** 100

C_MASK = 0
C_ID = C_MASK + SEQ
C_DELTA = C_ID + P
C_DESC = C_DELTA + E
C_POW = C_DESC + E
C_W = C_POW + NG * NT

A_Q, A_K, A_V = 0, D, 2 * D
A_R = 3 * D
A_BQ = A_R + E
A_BK = A_BQ + 1
A_W = A_BK + 1


def shape_constants():
    c = np.zeros((P, C_W), np.float32)
    j, i = np.arange(P)[:, None], np.arange(SEQ)[None, :]
    decay = np.float32(ALPHA) ** np.maximum(i - j, 0).astype(np.float32)
    c[:, C_MASK:C_ID] = np.where(i >= j, decay / np.float32(np.sqrt(D)), 0)
    c[:, C_ID:C_DELTA] = np.eye(P)
    c[:, C_DELTA:C_DESC] = np.arange(P)[:, None] % E == np.arange(E)[None, :]
    c[:, C_DESC:C_POW] = E - np.arange(E)
    c[:, C_POW:] = -0.5
    return c


def wait(eng, sem, value):
    if isinstance(value, int) and value <= 0:
        return
    eng.wait_ge(sem, value)


def build(nc, x_d, wattn_d, bvr_d, w1_d, w2_d, b12_d, const_d, out_d):
    with ExitStack() as ctx:
        def sb(name, shape, dt=F32):
            return ctx.enter_context(nc.sbuf_tensor(name, shape, dt))

        def ps(name, shape=(P, GT), dt=F32):
            return ctx.enter_context(nc.psum_tensor(name, list(shape), dt))

        def sem(name):
            return ctx.enter_context(nc.semaphore(name))

        const = sb("const", [P, C_W])
        ident_bf = sb("ident_bf", [P, P], BF16)
        wattn = sb("wattn", [P, A_W])
        w1 = sb("w1", [P, E * H])
        w1_hi = sb("w1_hi", [P, E * H], F32R)
        w1_lo = sb("w1_lo", [P, E * H], F32R)
        w2 = sb("w2", [P, NB * D])
        w2_hi = sb("w2_hi", [P, NB * D], F32R)
        w2_lo = sb("w2_lo", [P, NB * D], F32R)
        row_w = sb("row_w", [P, VW])
        row_b = sb("row_b", [P, VW])
        g_hi = sb("g_hi", [P, D], F32R)
        g_lo = sb("g_lo", [P, D], F32R)
        u_col = sb("u_col", [P, 1])
        bqk = sb("bqk", [P, 1])
        ones = sb("ones", [P, P])
        b12 = sb("b12", [P, H + D])
        b12_rest = sb("b12_rest", [P, H + D])
        b12_rest2 = sb("b12_rest2", [P, H + D])
        b_part1 = sb("b_part1", [P, H + D], BF16)
        b_part2 = sb("b_part2", [P, H + D], BF16)
        b_part3 = sb("b_part3", [P, H + D], BF16)
        b_rows = sb("b_rows", [P, H + D], BF16)
        mask_w = sb("mask_w", [P, E, H], BF16)
        x = sb("x", [P, TOK])
        xT_hi = sb("xT_hi", [P, TOK], F32R)
        xT_lo = sb("xT_lo", [P, TOK], F32R)
        route = sb("route", [P, TOK], BF16)
        attT = sb("attT", [P, TOK])
        stats = sb("stats", [P, NG * NT, 6])
        mv = sb("mv", [P, NG * NT, 2])
        var_eps = sb("var_eps", [P, NG * NT])
        rstd = sb("rstd", [P, NG * NT])
        out_rows = sb("out_rows", [P, TOK])
        xn = sb("xn", [P, NT, D])
        xT = sb("xT", [P, NT, P])
        rows = sb("rows", [P, NT, VW])
        v_hi = sb("v_hi", [P, NS, D], F32R)
        v_lo = sb("v_lo", [P, NS, D], F32R)
        keyT = sb("keyT", [P, NT, P])
        keyT_hi = sb("keyT_hi", [P, NS, P], F32R)
        keyT_lo = sb("keyT_lo", [P, NS, P], F32R)
        top = sb("top", [P, NT])
        is_top = sb("is_top", [P, NT, E])
        rank = sb("rank", [P, NT, E])
        top_rank = sb("top_rank", [P, NT])
        onehot = sb("onehot", [P, NT, 4, E], BF16)
        sc0 = sb("sc0", [P, NS, SEQ])
        sc0_hi = sb("sc0_hi", [P, NS, SEQ], F32R)
        sc0_lo = sb("sc0_lo", [P, NS, SEQ], F32R)
        sc1 = sb("sc1", [P, NS, P])
        finT = sb("finT", [P, NT, P])
        RH = 4
        hid_hi = sb("hid_hi", [P, RH, GT], F32R)
        hid_lo = sb("hid_lo", [P, RH, GT], F32R)

        RP = 2
        ps_hid = [ps(f"ps_hid{i}") for i in range(RP)]
        ps_y = ps("ps_y")
        ps_xk = ps("ps_xk")
        ps_a = ps("ps_a")
        ps_b = ps("ps_b")
        ps_att = ps("ps_att")
        ps_out = ps("ps_out")

        x0_in, xrest_in, wattn_in, bvr_in, w1_in, w2_in, const_in, b12_in = [
            sem(n) for n in ("x0_in", "xrest_in", "wattn_in", "bvr_in", "w1_in", "w2_in", "const_in", "b12_in")]
        b12_clear, b_split, b_laid, mask_ready = [sem(n) for n in ("b12_clear", "b_split", "b_laid", "mask_ready")]
        ones_ready, bqk_ready, setup_mm, rowb_c, rowb_ready = [
            sem(n) for n in ("ones_ready", "bqk_ready", "setup_mm", "rowb_c", "rowb_ready")]
        g_hi_ready, g_lo_ready, roww_ready, u_ready, ident_ready = [
            sem(n) for n in ("g_hi_ready", "g_lo_ready", "roww_ready", "u_ready", "ident_ready")]
        w1_hi_ready, w1_lo_ready, w2_hi_ready, w2_lo_ready = [
            sem(n) for n in ("w1_hi_ready", "w1_lo_ready", "w2_hi_ready", "w2_lo_ready")]
        stats_step = sem("stats_step")
        eps_ready = sem("eps_ready")
        rstd_ready = sem("rstd_ready")
        xn_ready = sem("xn_ready")
        xT_mm = sem("xT_mm")
        xT_ready = sem("xT_ready")
        xT_hi_ready = sem("xT_hi_ready")
        xT_lo_ready = sem("xT_lo_ready")
        rows_mm = sem("rows_mm")
        rows_ready = sem("rows_ready")
        v_hi_ready = sem("v_hi_ready")
        v_lo_ready = sem("v_lo_ready")
        key_mm = sem("key_mm")
        key_ready = sem("key_ready")
        key_hi_ready = sem("key_hi_ready")
        key_lo_ready = sem("key_lo_ready")
        argmax_step = sem("argmax_step")
        onehot_ready = sem("onehot_ready")
        route_mm = sem("route_mm")
        route_ready = sem("route_ready")
        sc_mm = sem("sc_mm")
        sc_ready = sem("sc_ready")
        sc_hi_ready = sem("sc_hi_ready")
        sc_lo_ready = sem("sc_lo_ready")
        att_mm = sem("att_mm")
        att_ready = sem("att_ready")
        fin_ready = sem("fin_ready")
        out_mm = sem("out_mm")
        out_ready = sem("out_ready")
        out_stored = sem("out_stored")
        hid_mm = sem("hid_mm")
        hid_hi_ready = sem("hid_hi_ready")
        hid_lo_ready = sem("hid_lo_ready")
        hid_used = sem("hid_used")

        def cols(t, n):
            return t[:, bass.ts(n, GT)]

        block = ctx.enter_context(nc.Block())

        @block.sync
        def _(sp):
            sp.dma_start(x[:, 0:GT], x_d[:, 0:GT]).then_inc(x0_in, 16)
            sp.dma_start(const[:], const_d).then_inc(const_in, 16)
            sp.dma_start(w1[:], w1_d).then_inc(w1_in, 16)
            sp.dma_start(x[:, GT:], x_d[:, GT:]).then_inc(xrest_in, 16)
            with sp.Fori(0, NG) as n:
                sp.wait_ge(out_ready, n + 2)
                sp.dma_start(cols(out_d, n), cols(out_rows, n)).then_inc(out_stored, 16)
            sp.wait_ge(out_stored, 16 * NG)

        @block.gpsimd
        def _(pool):
            for q in range(1, 4):
                pool.dma_start(b12[q * E:(q + 1) * E, :], b12_d).then_inc(b12_in, 16)
            pool.dma_start(row_b[:, 0:D + E], bvr_d.partition_broadcast(P)).then_inc(bvr_in, 16)
            pool.memset(ones[:], 1.0).then_inc(ones_ready, 1)
            pool.memset(b12[0:E, :], 0.0).then_inc(b12_clear, 1)

            def norm_scale(k, tiles):
                pool.wait_ge(stats_step, 2 * k + 2)
                pool.tensor_scalar(var_eps[:, tiles], mv[:, tiles, 1], EPS, None, ALU.add).then_inc(eps_ready, 1)
                pool.wait_ge(eps_ready, k + 1)
                pool.tensor_tensor(rstd[:, tiles], var_eps[:, tiles], const[:, C_POW:][:, tiles],
                                   ALU.pow).then_inc(rstd_ready, 1)

            def split_values(n):
                wait(pool, v_hi_ready, n + 1)
                wait(pool, att_mm, n)
                pool.tensor_tensor(v_lo[:], rows[:, 0:NT:2, 0:D], v_hi[:].bitcast(F32),
                                   ALU.subtract).then_inc(v_lo_ready, 1)

            def split_keys(n):
                wait(pool, key_hi_ready, n + 1)
                wait(pool, sc_mm, n)
                pool.tensor_tensor(keyT_lo[:], keyT[:, 0:NT:2, :], keyT_hi[:].bitcast(F32),
                                   ALU.subtract).then_inc(key_lo_ready, 1)

            def split_scores(n):
                wait(pool, sc_hi_ready, n + 1)
                wait(pool, att_mm, n)
                pool.tensor_tensor(sc0_lo[:], sc0[:], sc0_hi[:].bitcast(F32),
                                   ALU.subtract).then_inc(sc_lo_ready, 1)

            pool.wait_ge(const_in, 16)
            norm_scale(0, slice(0, NT))
            pool.wait_ge(b12_in, 16 * 3)
            pool.wait_ge(b12_clear, 1)
            pool.tensor_copy(b_part1[:], b12[:]).then_inc(b_split, 1)
            pool.wait_ge(b_split, 1)
            pool.tensor_tensor(b12_rest[:], b12[:], b_part1[:], ALU.subtract).then_inc(b_split, 1)
            pool.wait_ge(b_split, 2)
            pool.tensor_copy(b_part2[:], b12_rest[:]).then_inc(b_split, 1)
            pool.wait_ge(b_split, 3)
            pool.tensor_tensor(b12_rest2[:], b12_rest[:], b_part2[:], ALU.subtract).then_inc(b_split, 1)
            pool.wait_ge(b_split, 4)
            pool.tensor_copy(b_part3[:], b12_rest2[:]).then_inc(b_split, 1)
            pool.wait_ge(b_split, 5)
            pool.memset(b_rows[0:E, 0:H], BIG).then_inc(b_laid, 1)
            pool.memset(b_rows[0:E, H:], 0.0).then_inc(b_laid, 1)
            pool.tensor_copy(b_rows[E:2 * E, :], b_part1[E:2 * E, :]).then_inc(b_laid, 1)
            pool.tensor_copy(b_rows[2 * E:3 * E, :], b_part2[2 * E:3 * E, :]).then_inc(b_laid, 1)
            pool.tensor_copy(b_rows[3 * E:4 * E, :], b_part3[3 * E:4 * E, :]).then_inc(b_laid, 1)
            pool.wait_ge(b_laid, 5)
            pool.tensor_tensor(mask_w[:], b_rows[:, 0:H].unsqueeze(1).broadcast_to([P, E, H]),
                               const[:, C_DELTA:C_DESC].unsqueeze(2).broadcast_to([P, E, H]),
                               ALU.mult).then_inc(mask_ready, 1)
            norm_scale(1, slice(NT, NG * NT))
            split_values(0)
            split_keys(0)
            split_scores(0)
            pool.wait_ge(w2_hi_ready, 1)
            pool.tensor_tensor(w2_lo[:], w2[:], w2_hi[:].bitcast(F32), ALU.subtract).then_inc(w2_lo_ready, 1)
            with pool.Fori(0, NG - 1) as g:
                split_values(g + 1)
                split_keys(g + 1)
                split_scores(g + 1)

        @block.scalar
        def _(act):
            act.dma_start(wattn[:], wattn_d).then_inc(wattn_in, 16)
            act.dma_start(w2[:], w2_d).then_inc(w2_in, 16)

            def hidden_hi(g, b):
                wait(act, hid_mm, g * NB + b + 1)
                wait(act, hid_used, g * NB + b + 1)
                act.activation(hid_hi[:, b % RH, :], ps_hid[b % RP][:], ACT.Relu).then_inc(hid_hi_ready, 1)

            def evacuate_x(n):
                wait(act, xT_mm, n + 1)
                wait(act, sc_mm, n)
                act.activation(xT[:], ps_xk[:], ACT.Copy).then_inc(xT_ready, 1)
                act.activation(cols(xT_hi, n), ps_xk[:], ACT.Copy).then_inc(xT_hi_ready, 1)

            def value_hi(n):
                wait(act, rows_ready, 2 * n + 2)
                wait(act, att_mm, n)
                act.activation(v_hi[:], rows[:, 0:NT:2, 0:D], ACT.Copy).then_inc(v_hi_ready, 1)

            def evacuate_keys(n):
                wait(act, key_mm, n + 1)
                wait(act, sc_mm, n)
                wait(act, key_lo_ready, n)
                if isinstance(n, int) and n == 0:
                    act.wait_ge(u_ready, 1)
                act.activation(keyT[:], ps_xk[:], ACT.Identity, bias=u_col[:]).then_inc(key_ready, 1)
                act.activation(keyT_hi[:], ps_xk[:].rearrange("p (t k) -> p t k", t=NT)[:, 0:NT:2, :],
                               ACT.Identity, bias=u_col[:]).then_inc(key_hi_ready, 1)

            def evacuate_route(n):
                wait(act, route_mm, n + 1)
                act.activation(cols(route, n), ps_out[:, 0:GT // 2].bitcast(BF16), ACT.Copy).then_inc(route_ready, 1)

            def scores_hi(n):
                wait(act, sc_ready, n + 1)
                wait(act, att_mm, n)
                act.activation(sc0_hi[:], sc0[:], ACT.Copy).then_inc(sc_hi_ready, 1)

            def evacuate_attention(n):
                wait(act, att_mm, n + 1)
                act.activation(cols(attT, n), ps_att[:], ACT.Copy).then_inc(att_ready, 1)

            act.wait_ge(setup_mm, 1)
            act.activation(u_col[:], ps_out[:, D:D + 1], ACT.Copy).then_inc(u_ready, 1)
            act.activation(row_w[:, D + E:VW], ps_out[:, D + 1:D + 2], ACT.Copy).then_inc(roww_ready, 1)
            act.activation(row_w[:, 0:D + E], wattn[:, A_V:A_BQ], ACT.Copy).then_inc(roww_ready, 1)
            act.activation(row_b[:, D + E:VW], ps_out[:, D + 2:D + 3], ACT.Copy).then_inc(rowb_c, 1)
            act.activation(g_hi[:], ps_out[:, 0:D], ACT.Copy).then_inc(g_hi_ready, 1)
            evacuate_x(0)
            act.wait_ge(w1_in, 16)
            act.activation(w1_hi[:], w1[:], ACT.Copy).then_inc(w1_hi_ready, 1)
            value_hi(0)
            evacuate_keys(0)
            evacuate_route(0)
            scores_hi(0)
            act.wait_ge(w2_in, 16)
            act.activation(w2_hi[:], w2[:], ACT.Copy).then_inc(w2_hi_ready, 1)
            hidden_hi(0, 0)
            evacuate_attention(0)
            hidden_hi(0, 1)
            with act.Fori(0, NG - 1) as g:
                n = g + 1
                hidden_hi(g, 2)
                hidden_hi(g, 3)
                evacuate_x(n)
                hidden_hi(g, 4)
                value_hi(n)
                hidden_hi(g, 5)
                evacuate_keys(n)
                hidden_hi(g, 6)
                evacuate_route(n)
                scores_hi(n)
                hidden_hi(g, 7)
                hidden_hi(n, 0)
                evacuate_attention(n)
                hidden_hi(n, 1)
            for b in range(2, NB):
                hidden_hi(NG - 1, b)

        @block.vector
        def _(dve):
            def hidden_lo(g, b):
                wait(dve, hid_hi_ready, g * NB + b + 1)
                dve.scalar_tensor_tensor(hid_lo[:, b % RH, :], ps_hid[b % RP][:], 0.0,
                                         hid_hi[:, b % RH, :].bitcast(F32), ALU.max,
                                         ALU.subtract).then_inc(hid_lo_ready, 1)

            def norm_stats(k, tiles):
                for t in tiles:
                    last = dve.bn_stats(stats[:, t, :], x[:, t * P:(t + 1) * P])
                last.then_inc(stats_step, 1)
                dve.wait_ge(stats_step, 2 * k + 1)
                for t in tiles:
                    last = dve.bn_aggr(mv[:, t, :], stats[:, t, :])
                last.then_inc(stats_step, 1)

            def norm_apply(n):
                wait(dve, xT_mm, n)
                for t in range(NT):
                    last = dve.tensor_scalar(xn[:, t, :], x[:, bass.ds(n * GT + t * P, P)],
                                             mv[:, bass.ds(n * NT + t, 1), 0],
                                             rstd[:, bass.ds(n * NT + t, 1)], ALU.subtract, ALU.mult)
                last.then_inc(xn_ready, 1)

            def split_x(n):
                wait(dve, xT_hi_ready, n + 1)
                dve.tensor_tensor(cols(xT_lo, n), ps_xk[:], cols(xT_hi, n).bitcast(F32),
                                  ALU.subtract).then_inc(xT_lo_ready, 1)

            def evacuate_rows(n):
                wait(dve, rows_mm, n + 1)
                wait(dve, att_mm, n)
                wait(dve, v_lo_ready, n)
                for k, bank in enumerate((ps_a, ps_b)):
                    dve.tensor_tensor(rows[:, 2 * k:2 * k + 2, :],
                                      bank[:].rearrange("p (t c) -> p t c", t=2)[:, :, 0:VW],
                                      row_b[:].unsqueeze(1).broadcast_to([P, 2, VW]),
                                      ALU.add).then_inc(rows_ready, 1)

            def argmax(n):
                logits = rows[:, :, D:D + E]
                wait(dve, rows_ready, 2 * n + 2)
                dve.tensor_reduce(top[:], logits, AX.X, ALU.max).then_inc(argmax_step, 1)
                wait(dve, argmax_step, 5 * n + 1)
                dve.tensor_tensor(is_top[:], logits, top[:].unsqueeze(2).broadcast_to([P, NT, E]),
                                  ALU.is_equal).then_inc(argmax_step, 1)
                wait(dve, argmax_step, 5 * n + 2)
                dve.tensor_tensor(rank[:], is_top[:],
                                  const[:, C_DESC:C_POW].unsqueeze(1).broadcast_to([P, NT, E]),
                                  ALU.mult).then_inc(argmax_step, 1)
                wait(dve, argmax_step, 5 * n + 3)
                dve.tensor_reduce(top_rank[:], rank[:], AX.X, ALU.max).then_inc(argmax_step, 1)
                wait(dve, argmax_step, 5 * n + 4)
                wait(dve, route_mm, n)
                for q in range(1, 4):
                    last = dve.tensor_tensor(onehot[:, :, q, :], rank[:],
                                             top_rank[:].unsqueeze(2).broadcast_to([P, NT, E]), ALU.is_equal)
                last.then_inc(argmax_step, 1)
                wait(dve, argmax_step, 5 * n + 5)
                dve.tensor_scalar(onehot[:, :, 0, :], onehot[:, :, 1, :], -1.0, None,
                                  ALU.add).then_inc(onehot_ready, 1)

            def mask_scores(n):
                wait(dve, sc_mm, n + 1)
                wait(dve, att_mm, n)
                wait(dve, sc_lo_ready, n)
                for s in range(NS):
                    dve.scalar_tensor_tensor(sc0[:, s, :], ps_a[:, s * SEQ:(s + 1) * SEQ],
                                             rows[:, 2 * s, D + E:VW], const[:, C_MASK:C_MASK + SEQ],
                                             ALU.add, ALU.mult)
                for s in range(NS):
                    last = dve.scalar_tensor_tensor(sc1[:, s, :], ps_b[:, s * P:(s + 1) * P],
                                                    rows[:, 2 * s + 1, D + E:VW], const[:, C_MASK:C_MASK + P],
                                                    ALU.add, ALU.mult)
                last.then_inc(sc_ready, 1)

            def combine(g):
                wait(dve, hid_used, RH + NB * (g + 1))
                wait(dve, att_ready, g + 1)
                wait(dve, out_mm, g + 1)
                dve.scalar_tensor_tensor(finT[:], ps_y[:], 0.0, cols(attT, g), ALU.max,
                                         ALU.add).then_inc(fin_ready, 1)

            def add_residual(g):
                wait(dve, out_mm, g + 2)
                dve.tensor_tensor(cols(out_rows, g), ps_out[:], cols(x, g), ALU.add).then_inc(out_ready, 1)

            dve.wait_ge(x0_in, 16)
            norm_stats(0, range(NT))
            dve.wait_ge(wattn_in, 16)
            dve.tensor_tensor(bqk[:], wattn[:, A_BQ:A_BK], wattn[:, A_BK:A_W], ALU.mult).then_inc(bqk_ready, 1)
            dve.wait_ge(const_in, 16)
            dve.tensor_copy(ident_bf[:], const[:, C_ID:C_DELTA]).then_inc(ident_ready, 1)
            dve.wait_ge(rstd_ready, 1)
            norm_apply(0)
            dve.wait_ge(g_hi_ready, 1)
            dve.tensor_tensor(g_lo[:], ps_out[:, 0:D], g_hi[:].bitcast(F32), ALU.subtract).then_inc(g_lo_ready, 1)
            split_x(0)
            dve.wait_ge(xrest_in, 16)
            norm_stats(1, range(NT, NG * NT))
            dve.wait_ge(w1_hi_ready, 1)
            dve.tensor_tensor(w1_lo[:], w1[:], w1_hi[:].bitcast(F32), ALU.subtract).then_inc(w1_lo_ready, 1)
            dve.wait_ge(bvr_in, 16)
            dve.wait_ge(rowb_c, 1)
            evacuate_rows(0)
            argmax(0)
            mask_scores(0)
            dve.sem_inc(hid_lo_ready, RP)
            dve.sem_inc(fin_ready, 1)
            dve.sem_inc(out_ready, 1)
            hidden_lo(0, 0)
            hidden_lo(0, 1)
            dve.wait_ge(rstd_ready, 2)
            with dve.Fori(0, NG - 1) as g:
                n = g + 1
                hidden_lo(g, 2)
                norm_apply(n)
                hidden_lo(g, 3)
                split_x(n)
                hidden_lo(g, 4)
                evacuate_rows(n)
                hidden_lo(g, 5)
                argmax(n)
                hidden_lo(g, 6)
                mask_scores(n)
                hidden_lo(g, 7)
                hidden_lo(n, 0)
                combine(g)
                hidden_lo(n, 1)
                add_residual(g)
            for b in range(2, NB):
                hidden_lo(NG - 1, b)
            combine(NG - 1)
            add_residual(NG - 1)

        @block.tensor
        def _(pe):
            ident = const[:, C_ID:C_DELTA]

            def hidden(g, b):
                w = slice(b * P, (b + 1) * P)
                acc = ps_hid[b % RP][:]
                wait(pe, hid_lo_ready, g * NB + b + 1)
                wait(pe, xT_lo_ready, g + 1)
                pe.matmul(acc, w1_hi[:, w], cols(xT_hi, g), start=True, stop=False)
                pe.matmul(acc, w1_hi[:, w], cols(xT_lo, g), start=False, stop=False)
                pe.matmul(acc, w1_lo[:, w], cols(xT_hi, g), start=False, stop=False)
                wait(pe, route_ready, g + 1)
                pe.matmul(acc, mask_w[:, b * EB:(b + 1) * EB, :], cols(route, g),
                          start=False, stop=True).then_inc(hid_mm, 1)

            def output(g, b):
                w = slice(b * D, (b + 1) * D)
                wait(pe, hid_lo_ready, g * NB + b + 1 + RP)
                if b == 0:
                    wait(pe, fin_ready, g + 1)
                if b == NB - 1:
                    pe.matmul(ps_y[:], b_rows[:, H:], cols(route, g), start=False, stop=False)
                pe.matmul(ps_y[:], w2_hi[:, w], hid_hi[:, b % RH, :], start=b == 0, stop=False)
                pe.matmul(ps_y[:], w2_lo[:, w], hid_hi[:, b % RH, :], start=False, stop=False)
                last = pe.matmul(ps_y[:], w2_hi[:, w], hid_lo[:, b % RH, :], start=False, stop=b == NB - 1)
                last.then_inc(hid_used, 1)

            def transpose_x(n):
                wait(pe, xn_ready, n + 1)
                wait(pe, key_hi_ready, n)
                for t in range(NT):
                    last = pe.transpose(ps_xk[:, t * P:(t + 1) * P], xn[:, t, :], ident)
                last.then_inc(xT_mm, 1)

            def row_products(n):
                wait(pe, xT_ready, n + 1)
                wait(pe, sc_ready, n)
                for t in range(NT):
                    bank = (ps_a, ps_b)[t // 2]
                    last = pe.matmul(bank[:, (t % 2) * SEQ:(t % 2) * SEQ + VW], xT[:, t, :], row_w[:],
                                     start=True, stop=True)
                last.then_inc(rows_mm, 1)

            def key_products(n):
                wait(pe, xT_lo_ready, n + 1)
                wait(pe, xT_ready, n + 1)
                pe.matmul(ps_xk[:], g_hi[:], cols(xT_hi, n), start=True, stop=False)
                pe.matmul(ps_xk[:], g_hi[:], cols(xT_lo, n), start=False, stop=False)
                pe.matmul(ps_xk[:], g_lo[:], cols(xT_hi, n), start=False, stop=True).then_inc(key_mm, 1)

            def transpose_route(n):
                wait(pe, onehot_ready, n + 1)
                wait(pe, out_ready, n)
                for t in range(NT):
                    last = pe.transpose(ps_out[:, t * (P // 2):(t + 1) * (P // 2)].bitcast(BF16),
                                        onehot[:, t].rearrange("p q e -> p (q e)"), ident_bf[:])
                last.then_inc(route_mm, 1)

            def score_products(n):
                wait(pe, key_lo_ready, n + 1)
                wait(pe, rows_ready, 2 * n + 2)
                for s in range(NS):
                    xs_hi = xT_hi[:, bass.ds(n * GT + s * SEQ, SEQ)]
                    xs_lo = xT_lo[:, bass.ds(n * GT + s * SEQ, SEQ)]
                    acc = ps_a[:, s * SEQ:(s + 1) * SEQ]
                    pe.matmul(acc, keyT_hi[:, s, :], xs_hi, start=True, stop=False)
                    pe.matmul(acc, keyT_hi[:, s, :], xs_lo, start=False, stop=False)
                    pe.matmul(acc, keyT_lo[:, s, :], xs_hi, start=False, stop=True)
                for s in range(NS):
                    last = pe.matmul(ps_b[:, s * P:(s + 1) * P], keyT[:, 2 * s + 1, :], xT[:, 2 * s + 1, :],
                                     start=True, stop=True)
                last.then_inc(sc_mm, 1)

            def attention_products(n):
                wait(pe, sc_lo_ready, n + 1)
                wait(pe, v_lo_ready, n + 1)
                wait(pe, att_ready, n)
                for s in range(NS):
                    acc = ps_att[:, s * SEQ:(s + 1) * SEQ]
                    pe.matmul(acc, v_hi[:, s, :], sc0_hi[:, s, :], start=True, stop=False)
                    pe.matmul(acc, v_hi[:, s, :], sc0_lo[:, s, :], start=False, stop=False)
                    pe.matmul(acc, v_lo[:, s, :], sc0_hi[:, s, :], start=False, stop=False)
                    last = pe.matmul(ps_att[:, s * SEQ + P:(s + 1) * SEQ], rows[:, 2 * s + 1, 0:D], sc1[:, s, :],
                                     start=False, stop=True)
                last.then_inc(att_mm, 1)

            def transpose_output(g):
                wait(pe, fin_ready, g + 2)
                wait(pe, route_ready, g + 1)
                for t in range(NT):
                    last = pe.transpose(ps_out[:, t * P:(t + 1) * P], finT[:, t, :], ident)
                last.then_inc(out_mm, 1)

            pe.wait_ge(wattn_in, 16)
            wq, wk = wattn[:, A_Q:A_K], wattn[:, A_K:A_V]
            pe.matmul(ps_out[:, 0:D], wk, wq, start=True, stop=True)
            pe.matmul(ps_out[:, D:D + 1], wq, wattn[:, A_BK:A_W], start=True, stop=True)
            pe.matmul(ps_out[:, D + 1:D + 2], wk, wattn[:, A_BQ:A_BK], start=True, stop=True)
            pe.wait_ge(bqk_ready, 1)
            pe.wait_ge(ones_ready, 1)
            pe.matmul(ps_out[:, D + 2:D + 3], ones[:], bqk[:], start=True, stop=True).then_inc(setup_mm, 1)
            pe.sem_inc(hid_used, RH)
            pe.sem_inc(out_mm, 1)
            pe.wait_ge(const_in, 16)
            transpose_x(0)
            pe.wait_ge(roww_ready, 2)
            row_products(0)
            pe.wait_ge(g_lo_ready, 1)
            key_products(0)
            score_products(0)
            pe.wait_ge(ident_ready, 1)
            transpose_route(0)
            pe.wait_ge(w1_lo_ready, 1)
            pe.wait_ge(mask_ready, 1)
            hidden(0, 0)
            attention_products(0)
            hidden(0, 1)
            pe.wait_ge(w2_lo_ready, 1)
            with pe.Fori(0, NG - 1) as g:
                n = g + 1
                hidden(g, 2)
                output(g, 0)
                hidden(g, 3)
                output(g, 1)
                transpose_x(n)
                hidden(g, 4)
                output(g, 2)
                row_products(n)
                hidden(g, 5)
                output(g, 3)
                key_products(n)
                hidden(g, 6)
                output(g, 4)
                score_products(n)
                transpose_route(n)
                hidden(g, 7)
                output(g, 5)
                output(g, 6)
                hidden(n, 0)
                output(g, 7)
                attention_products(n)
                hidden(n, 1)
                transpose_output(g)
            for b in range(2, NB):
                hidden(NG - 1, b)
                output(NG - 1, b - 2)
            output(NG - 1, NB - 2)
            output(NG - 1, NB - 1)
            transpose_output(NG - 1)


def kernel(L0_attn_x, L0_attn_W_qkv, L0_attn_b_qkv, L0_ffn_router_w, L0_ffn_router_b,
           L0_ffn_weights1, L0_ffn_bias1, L0_ffn_weights2, L0_ffn_bias2):
    import concourse.bacc as bacc
    from concourse.bass_utils import run_bass_kernel_spmd

    xs, w, b = np.asarray(L0_attn_x), np.asarray(L0_attn_W_qkv), np.asarray(L0_attn_b_qkv)
    wq, wk, wv = w[0:D], w[D:2 * D], w[2 * D:]
    data = {
        "in_x": xs.reshape(TOK // P, P, D).transpose(1, 0, 2).reshape(P, TOK),
        "in_wattn": np.concatenate([wq, wk, wv.T, np.asarray(L0_ffn_router_w).T,
                                    b[0:D, None], b[D:2 * D, None]], axis=1),
        "in_bvr": np.concatenate([b[2 * D:], np.asarray(L0_ffn_router_b)]),
        "in_w1": np.asarray(L0_ffn_weights1).transpose(1, 0, 2).reshape(D, E * H),
        "in_w2": np.asarray(L0_ffn_weights2).reshape(NB, P, D).transpose(1, 0, 2).reshape(P, NB * D),
        "in_b12": np.concatenate([np.asarray(L0_ffn_bias1), np.asarray(L0_ffn_bias2)], axis=1),
        "in_const": shape_constants(),
    }
    data = {k: np.ascontiguousarray(v) for k, v in data.items()}
    nc = bacc.Bacc("TRN2", target_bir_lowering=False, num_devices=1)
    aps = [nc.dram_tensor(k, v.shape, mybir.dt.from_np(v.dtype), kind="ExternalInput").ap()
           for k, v in data.items()]
    out = nc.dram_tensor("out_rows_d", (P, TOK), F32, kind="ExternalOutput").ap()
    build(nc, *aps, out)
    got = run_bass_kernel_spmd(nc, [data], core_ids=[0]).results[0]["out_rows_d"]
    return got.reshape(P, TOK // P, D).transpose(1, 0, 2).reshape(BATCH, SEQ, D)
```

```python
from contextlib import ExitStack

import numpy as np

import concourse.bass as bass
from concourse import mybir

F32 = mybir.dt.float32
F32R = mybir.dt.float32r
BF16 = mybir.dt.bfloat16
ALU = mybir.AluOpType
ACT = mybir.ActivationFunctionType
AX = mybir.AxisListType

P = 128
D = 128
SEQ = 256
BATCH = 8
TOK = BATCH * SEQ
GT = 512
NG = TOK // GT
NT = GT // P
NS = GT // SEQ
E = 32
H = 32
EB = P // H
NB = E // EB
VW = D + E + 1
ALPHA = 0.99
EPS = 1e-5
W1_FIRST = 2 * P
BIG = 2.0 ** 100

C_MASK = 0
C_ID = C_MASK + SEQ
C_DELTA = C_ID + P
C_DESC = C_DELTA + E
C_POW = C_DESC + E
C_W = C_POW + NG * NT

A_Q, A_K, A_V = 0, D, 2 * D
A_R = 3 * D
A_BQ = A_R + E
A_BK = A_BQ + 1
A_W = A_BK + 1


def shape_constants():
    c = np.zeros((P, C_W), np.float32)
    j, i = np.arange(P)[:, None], np.arange(SEQ)[None, :]
    decay = np.float32(ALPHA) ** np.maximum(i - j, 0).astype(np.float32)
    c[:, C_MASK:C_ID] = np.where(i >= j, decay / np.float32(np.sqrt(D)), 0)
    c[:, C_ID:C_DELTA] = np.eye(P)
    c[:, C_DELTA:C_DESC] = np.arange(P)[:, None] % E == np.arange(E)[None, :]
    c[:, C_DESC:C_POW] = E - np.arange(E)
    c[:, C_POW:] = -0.5
    return c


def wait(eng, sem, value):
    if isinstance(value, int) and value <= 0:
        return
    eng.wait_ge(sem, value)


def build(nc, x_d, xT_d, wattn_d, bvr_d, w1_d, w2_d, b12_d, const_d, out_d):
    with ExitStack() as ctx:
        def sb(name, shape, dt=F32):
            return ctx.enter_context(nc.sbuf_tensor(name, shape, dt))

        def ps(name, shape=(P, GT), dt=F32):
            return ctx.enter_context(nc.psum_tensor(name, list(shape), dt))

        def sem(name):
            return ctx.enter_context(nc.semaphore(name))

        const = sb("const", [P, C_W])
        ident_bf = sb("ident_bf", [P, P], BF16)
        wattn = sb("wattn", [P, A_W])
        w1 = sb("w1", [P, E * H])
        w1_hi = sb("w1_hi", [P, E * H], F32R)
        w1_lo = sb("w1_lo", [P, E * H], F32R)
        w2 = sb("w2", [P, NB * D])
        w2_hi = sb("w2_hi", [P, NB * D], F32R)
        w2_lo = sb("w2_lo", [P, NB * D], F32R)
        row_w = sb("row_w", [P, VW])
        row_b = sb("row_b", [P, VW])
        g_hi = sb("g_hi", [P, D], F32R)
        g_lo = sb("g_lo", [P, D], F32R)
        u_col = sb("u_col", [P, 1])
        bqk = sb("bqk", [P, 1])
        ones = sb("ones", [P, P])
        b12 = sb("b12", [P, H + D])
        b12_rest = sb("b12_rest", [P, H + D])
        b12_rest2 = sb("b12_rest2", [P, H + D])
        b_rows = sb("b_rows", [P, H + D], BF16)
        mask_w = sb("mask_w", [P, E, H], BF16)
        x = sb("x", [P, TOK])
        xT_hi = sb("xT_hi", [P, TOK], F32R)
        xT_lo = sb("xT_lo", [P, TOK], F32R)
        route = sb("route", [P, TOK], BF16)
        x_byT = sb("x_byT", [P, TOK])
        attT = sb("attT", [P, TOK])
        stats = sb("stats", [P, NG * NT, 6])
        mv = sb("mv", [P, NG * NT, 2])
        var_eps = sb("var_eps", [P, NG * NT])
        rstd = sb("rstd", [P, NG * NT])
        outT = sb("outT", [P, TOK])
        xn = sb("xn", [P, NT, D])
        xT = sb("xT", [P, NT, P])
        rows = sb("rows", [P, NT, VW])
        v_hi = sb("v_hi", [P, NS, D], F32R)
        v_lo = sb("v_lo", [P, NS, D], F32R)
        keyT = sb("keyT", [P, NT, P])
        keyT_hi = sb("keyT_hi", [P, NS, P], F32R)
        keyT_lo = sb("keyT_lo", [P, NS, P], F32R)
        top = sb("top", [P, NT])
        is_top = sb("is_top", [P, NT, E])
        rank = sb("rank", [P, NT, E])
        top_rank = sb("top_rank", [P, NT])
        onehot = sb("onehot", [P, NT, 4, E], BF16)
        sc0 = sb("sc0", [P, NS, SEQ])
        sc0_hi = sb("sc0_hi", [P, NS, SEQ], F32R)
        sc0_lo = sb("sc0_lo", [P, NS, SEQ], F32R)
        sc1 = sb("sc1", [P, NS, P])
        RH = 4
        hid_hi = sb("hid_hi", [P, RH, GT], F32R)
        hid_lo = sb("hid_lo", [P, RH, GT], F32R)

        RP = 2
        ps_hid = [ps(f"ps_hid{i}") for i in range(RP)]
        ps_y = ps("ps_y")
        ps_xk = ps("ps_xk")
        ps_a = ps("ps_a")
        ps_b = ps("ps_b")
        ps_att = ps("ps_att")
        ps_route = ps("ps_route")

        x0_in, xrest_in, xT_in, wattn_in, bvr_in, w1_in, w2_in, const_in, b12_in = [
            sem(n) for n in ("x0_in", "xrest_in", "xT_in", "wattn_in", "bvr_in", "w1_in", "w2_in", "const_in",
                             "b12_in")]
        b_split, mask_ready = [sem(n) for n in ("b_split", "mask_ready")]
        ones_ready, bqk_ready, setup_mm, rowb_c, rowb_ready = [
            sem(n) for n in ("ones_ready", "bqk_ready", "setup_mm", "rowb_c", "rowb_ready")]
        g_hi_ready, g_lo_ready, roww_ready, u_ready, ident_ready = [
            sem(n) for n in ("g_hi_ready", "g_lo_ready", "roww_ready", "u_ready", "ident_ready")]
        w1_hi_ready, w1_first_ready, w1_lo_ready, w2_hi_ready, w2_lo_ready = [
            sem(n) for n in ("w1_hi_ready", "w1_first_ready", "w1_lo_ready", "w2_hi_ready", "w2_lo_ready")]
        stats_step = sem("stats_step")
        eps_ready = sem("eps_ready")
        rstd_ready = sem("rstd_ready")
        xn_ready = sem("xn_ready")
        xT_mm = sem("xT_mm")
        xT_ready = sem("xT_ready")
        xT_hi_ready = sem("xT_hi_ready")
        xT_lo_ready = sem("xT_lo_ready")
        rows_mm = sem("rows_mm")
        rows_ready = sem("rows_ready")
        v_hi_ready = sem("v_hi_ready")
        v_lo_ready = sem("v_lo_ready")
        key_mm = sem("key_mm")
        key_ready = sem("key_ready")
        key_hi_ready = sem("key_hi_ready")
        key_lo_ready = sem("key_lo_ready")
        argmax_step = sem("argmax_step")
        onehot_ready = sem("onehot_ready")
        route_mm = sem("route_mm")
        route_ready = sem("route_ready")
        sc_mm = sem("sc_mm")
        sc_ready = sem("sc_ready")
        sc_hi_ready = sem("sc_hi_ready")
        sc_lo_ready = sem("sc_lo_ready")
        att_mm = sem("att_mm")
        att_ready = sem("att_ready")
        out_ready = sem("out_ready")
        out_stored = sem("out_stored")
        hid_mm = sem("hid_mm")
        hid_hi_ready = sem("hid_hi_ready")
        hid_lo_ready = sem("hid_lo_ready")
        hid_used = sem("hid_used")

        def cols(t, n):
            return t[:, bass.ts(n, GT)]

        block = ctx.enter_context(nc.Block())

        @block.sync
        def _(sp):
            sp.dma_start(x[:, 0:GT], x_d[:, 0:GT]).then_inc(x0_in, 16)
            sp.dma_start(const[:], const_d).then_inc(const_in, 16)
            sp.dma_start(w1[:], w1_d).then_inc(w1_in, 16)
            sp.dma_start(x[:, GT:], x_d[:, GT:]).then_inc(xrest_in, 16)
            sp.dma_start(x_byT[:], xT_d).then_inc(xT_in, 16)
            with sp.Fori(0, NG) as n:
                sp.wait_ge(out_ready, n + 2)
                sp.dma_start(cols(out_d, n), cols(outT, n)).then_inc(out_stored, 16)
            sp.wait_ge(out_stored, 16 * NG)

        @block.gpsimd
        def _(pool):
            pool.dma_start(row_b[:, 0:D + E], bvr_d.partition_broadcast(P)).then_inc(bvr_in, 16)
            pool.memset(ones[:], 1.0).then_inc(ones_ready, 1)

            def norm_scale(k, tiles):
                pool.wait_ge(eps_ready, k + 1)
                pool.tensor_tensor(rstd[:, tiles], var_eps[:, tiles], const[:, C_POW:][:, tiles],
                                   ALU.pow).then_inc(rstd_ready, 1)

            def split_values(n):
                wait(pool, v_hi_ready, n + 1)
                wait(pool, att_mm, n)
                pool.tensor_tensor(v_lo[:], rows[:, 0:NT:2, 0:D], v_hi[:].bitcast(F32),
                                   ALU.subtract).then_inc(v_lo_ready, 1)

            def split_keys(n):
                wait(pool, key_hi_ready, n + 1)
                wait(pool, sc_mm, n)
                pool.tensor_tensor(keyT_lo[:], keyT[:, 0:NT:2, :], keyT_hi[:].bitcast(F32),
                                   ALU.subtract).then_inc(key_lo_ready, 1)

            def split_scores(n):
                wait(pool, sc_hi_ready, n + 1)
                wait(pool, att_mm, n)
                pool.tensor_tensor(sc0_lo[:], sc0[:], sc0_hi[:].bitcast(F32),
                                   ALU.subtract).then_inc(sc_lo_ready, 1)

            pool.wait_ge(const_in, 16)
            norm_scale(0, slice(0, NT))
            pool.wait_ge(b_split, 5)
            pool.tensor_tensor(mask_w[:], b_rows[:, 0:H].unsqueeze(1).broadcast_to([P, E, H]),
                               const[:, C_DELTA:C_DESC].unsqueeze(2).broadcast_to([P, E, H]),
                               ALU.mult).then_inc(mask_ready, 1)
            pool.wait_ge(w1_hi_ready, 2)
            pool.tensor_tensor(w1_lo[:, W1_FIRST:], w1[:, W1_FIRST:], w1_hi[:, W1_FIRST:].bitcast(F32),
                               ALU.subtract).then_inc(w1_lo_ready, 1)
            norm_scale(1, slice(NT, 2 * NT))
            split_keys(0)
            pool.wait_ge(w2_hi_ready, 1)
            pool.tensor_tensor(w2_lo[:], w2[:], w2_hi[:].bitcast(F32), ALU.subtract).then_inc(w2_lo_ready, 1)
            split_values(0)
            norm_scale(2, slice(2 * NT, NG * NT))
            split_scores(0)
            with pool.Fori(0, NG - 1) as g:
                split_values(g + 1)
                split_keys(g + 1)
                split_scores(g + 1)

        @block.scalar
        def _(act):
            act.dma_start(wattn[:], wattn_d).then_inc(wattn_in, 16)
            act.dma_start(b12[:], b12_d).then_inc(b12_in, 16)
            act.dma_start(w2[:], w2_d).then_inc(w2_in, 16)

            def hidden_hi(g, b):
                wait(act, hid_mm, g * NB + b + 1)
                wait(act, hid_used, g * NB + b + 1)
                act.activation(hid_hi[:, b % RH, :], ps_hid[b % RP][:], ACT.Relu).then_inc(hid_hi_ready, 1)

            def evacuate_x(n):
                wait(act, xT_mm, n + 1)
                wait(act, sc_mm, n)
                act.activation(xT[:], ps_xk[:], ACT.Copy).then_inc(xT_ready, 1)
                act.activation(cols(xT_hi, n), ps_xk[:], ACT.Copy).then_inc(xT_hi_ready, 1)

            def value_hi(n):
                wait(act, rows_ready, 2 * n + 2)
                wait(act, att_mm, n)
                act.activation(v_hi[:], rows[:, 0:NT:2, 0:D], ACT.Copy).then_inc(v_hi_ready, 1)

            def evacuate_keys(n):
                wait(act, key_mm, n + 1)
                wait(act, sc_mm, n)
                wait(act, key_lo_ready, n)
                if isinstance(n, int) and n == 0:
                    act.wait_ge(u_ready, 1)
                act.activation(keyT[:], ps_xk[:], ACT.Identity, bias=u_col[:]).then_inc(key_ready, 1)
                act.activation(keyT_hi[:], ps_xk[:].rearrange("p (t k) -> p t k", t=NT)[:, 0:NT:2, :],
                               ACT.Identity, bias=u_col[:]).then_inc(key_hi_ready, 1)

            def evacuate_route(n):
                wait(act, route_mm, n + 1)
                act.activation(cols(route, n), ps_route[:, 0:GT // 2].bitcast(BF16), ACT.Copy).then_inc(route_ready, 1)

            def scores_hi(n):
                wait(act, sc_ready, n + 1)
                wait(act, att_mm, n)
                act.activation(sc0_hi[:], sc0[:], ACT.Copy).then_inc(sc_hi_ready, 1)

            act.wait_ge(setup_mm, 1)
            act.activation(u_col[:], ps_route[:, D:D + 1], ACT.Copy).then_inc(u_ready, 1)
            act.activation(row_w[:, D + E:VW], ps_route[:, D + 1:D + 2], ACT.Copy).then_inc(roww_ready, 1)
            act.activation(row_w[:, 0:D + E], wattn[:, A_V:A_BQ], ACT.Copy).then_inc(roww_ready, 1)
            act.activation(row_b[:, D + E:VW], ps_route[:, D + 2:D + 3], ACT.Copy).then_inc(rowb_c, 1)
            act.activation(g_hi[:], ps_route[:, 0:D], ACT.Copy).then_inc(g_hi_ready, 1)
            act.wait_ge(w1_in, 16)
            act.activation(w1_hi[:, 0:W1_FIRST], w1[:, 0:W1_FIRST], ACT.Copy).then_inc(w1_hi_ready, 1)
            act.activation(w1_hi[:, W1_FIRST:], w1[:, W1_FIRST:], ACT.Copy).then_inc(w1_hi_ready, 1)
            evacuate_x(0)
            act.wait_ge(w2_in, 16)
            act.activation(w2_hi[:], w2[:], ACT.Copy).then_inc(w2_hi_ready, 1)
            value_hi(0)
            evacuate_keys(0)
            evacuate_route(0)
            hidden_hi(0, 0)
            hidden_hi(0, 1)
            scores_hi(0)
            with act.Fori(0, NG - 1) as g:
                n = g + 1
                hidden_hi(g, 2)
                hidden_hi(g, 3)
                hidden_hi(g, 4)
                evacuate_x(n)
                value_hi(n)
                hidden_hi(g, 5)
                evacuate_keys(n)
                hidden_hi(g, 6)
                hidden_hi(g, 7)
                evacuate_route(n)
                hidden_hi(n, 0)
                hidden_hi(n, 1)
                scores_hi(n)
            for b in range(2, NB):
                hidden_hi(NG - 1, b)

        @block.vector
        def _(dve):
            def hidden_lo(g, b):
                wait(dve, hid_hi_ready, g * NB + b + 1)
                dve.scalar_tensor_tensor(hid_lo[:, b % RH, :], ps_hid[b % RP][:], 0.0,
                                         hid_hi[:, b % RH, :].bitcast(F32), ALU.max,
                                         ALU.subtract).then_inc(hid_lo_ready, 1)

            def norm_stats(k, tiles):
                for t in tiles:
                    last = dve.bn_stats(stats[:, t, :], x[:, t * P:(t + 1) * P])
                last.then_inc(stats_step, 1)
                dve.wait_ge(stats_step, 2 * k + 1)
                for t in tiles:
                    last = dve.bn_aggr(mv[:, t, :], stats[:, t, :])
                last.then_inc(stats_step, 1)
                dve.wait_ge(stats_step, 2 * k + 2)
                tiles = slice(tiles.start, tiles.stop)
                dve.tensor_scalar(var_eps[:, tiles], mv[:, tiles, 1], EPS, None, ALU.add).then_inc(eps_ready, 1)

            def norm_apply(n):
                wait(dve, xT_mm, n)
                for t in range(NT):
                    dve.tensor_scalar(xn[:, t, :], x[:, bass.ds(n * GT + t * P, P)],
                                      mv[:, bass.ds(n * NT + t, 1), 0],
                                      rstd[:, bass.ds(n * NT + t, 1)], ALU.subtract,
                                      ALU.mult).then_inc(xn_ready, 1)

            def split_x(n):
                wait(dve, xT_hi_ready, n + 1)
                dve.tensor_tensor(cols(xT_lo, n), ps_xk[:], cols(xT_hi, n).bitcast(F32),
                                  ALU.subtract).then_inc(xT_lo_ready, 1)

            def evacuate_rows(n):
                wait(dve, rows_mm, n + 1)
                wait(dve, att_mm, n)
                wait(dve, v_lo_ready, n)
                for k, bank in enumerate((ps_a, ps_b)):
                    dve.tensor_tensor(rows[:, 2 * k:2 * k + 2, :],
                                      bank[:].rearrange("p (t c) -> p t c", t=2)[:, :, 0:VW],
                                      row_b[:].unsqueeze(1).broadcast_to([P, 2, VW]),
                                      ALU.add).then_inc(rows_ready, 1)

            def rank_top(n):
                logits = rows[:, :, D:D + E]
                wait(dve, rows_ready, 2 * n + 2)
                dve.tensor_reduce(top[:], logits, AX.X, ALU.max).then_inc(argmax_step, 1)
                wait(dve, argmax_step, 5 * n + 1)
                dve.tensor_tensor(is_top[:], logits, top[:].unsqueeze(2).broadcast_to([P, NT, E]),
                                  ALU.is_equal).then_inc(argmax_step, 1)
                wait(dve, argmax_step, 5 * n + 2)
                dve.tensor_tensor(rank[:], is_top[:],
                                  const[:, C_DESC:C_POW].unsqueeze(1).broadcast_to([P, NT, E]),
                                  ALU.mult).then_inc(argmax_step, 1)

            def one_hot(n):
                wait(dve, argmax_step, 5 * n + 3)
                dve.tensor_reduce(top_rank[:], rank[:], AX.X, ALU.max).then_inc(argmax_step, 1)
                wait(dve, argmax_step, 5 * n + 4)
                wait(dve, route_mm, n)
                dve.tensor_tensor(onehot[:, :, 1, :], rank[:], top_rank[:].unsqueeze(2).broadcast_to([P, NT, E]),
                                  ALU.is_equal).then_inc(argmax_step, 1)
                wait(dve, argmax_step, 5 * n + 5)
                dve.tensor_scalar(onehot[:, :, 0, :], onehot[:, :, 1, :], -1.0, None, ALU.add)
                dve.tensor_copy(onehot[:, :, 2:4, :], onehot[:, :, 1:2, :].broadcast_to([P, NT, 2, E]))\
                   .then_inc(onehot_ready, 1)

            def mask_scores(n):
                wait(dve, sc_mm, n + 1)
                wait(dve, att_mm, n)
                wait(dve, sc_lo_ready, n)
                for s in range(NS):
                    dve.scalar_tensor_tensor(sc0[:, s, :], ps_a[:, s * SEQ:(s + 1) * SEQ],
                                             rows[:, 2 * s, D + E:VW], const[:, C_MASK:C_MASK + SEQ],
                                             ALU.add, ALU.mult)
                for s in range(NS):
                    last = dve.scalar_tensor_tensor(sc1[:, s, :], ps_b[:, s * P:(s + 1) * P],
                                                    rows[:, 2 * s + 1, D + E:VW], const[:, C_MASK:C_MASK + P],
                                                    ALU.add, ALU.mult)
                last.then_inc(sc_ready, 1)

            def add_attention(n):
                wait(dve, att_mm, n + 1)
                dve.tensor_tensor(cols(attT, n), ps_att[:], cols(x_byT, n), ALU.add).then_inc(att_ready, 1)

            def combine(g):
                wait(dve, att_ready, g + 1)
                wait(dve, hid_used, RH + NB * (g + 1))
                dve.scalar_tensor_tensor(cols(outT, g), ps_y[:], 0.0, cols(attT, g), ALU.max,
                                         ALU.add).then_inc(out_ready, 1)

            dve.sem_inc(hid_lo_ready, RP)
            dve.sem_inc(out_ready, 1)
            dve.wait_ge(x0_in, 16)
            norm_stats(0, range(NT))
            dve.wait_ge(wattn_in, 16)
            dve.tensor_tensor(bqk[:], wattn[:, A_BQ:A_BK], wattn[:, A_BK:A_W], ALU.mult).then_inc(bqk_ready, 1)
            dve.wait_ge(b12_in, 16)
            dve.tensor_copy(b_rows[:], b12[:]).then_inc(b_split, 1)
            dve.wait_ge(b_split, 1)
            dve.tensor_tensor(b12_rest[:], b12[:], b_rows[:], ALU.subtract).then_inc(b_split, 1)
            dve.wait_ge(b_split, 2)
            dve.tensor_copy(b_rows[2 * E:, :], b12_rest[2 * E:, :]).then_inc(b_split, 1)
            dve.wait_ge(rstd_ready, 1)
            norm_apply(0)
            dve.wait_ge(b_split, 3)
            dve.tensor_tensor(b12_rest2[3 * E:, :], b12_rest[3 * E:, :], b_rows[3 * E:, :],
                              ALU.subtract).then_inc(b_split, 1)
            dve.wait_ge(b_split, 4)
            dve.tensor_copy(b_rows[3 * E:, :], b12_rest2[3 * E:, :]).then_inc(b_split, 1)
            dve.wait_ge(g_hi_ready, 1)
            dve.tensor_tensor(g_lo[:], ps_route[:, 0:D], g_hi[:].bitcast(F32), ALU.subtract).then_inc(g_lo_ready, 1)
            split_x(0)
            dve.wait_ge(w1_hi_ready, 1)
            dve.tensor_tensor(w1_lo[:, 0:W1_FIRST], w1[:, 0:W1_FIRST], w1_hi[:, 0:W1_FIRST].bitcast(F32),
                              ALU.subtract).then_inc(w1_first_ready, 1)
            dve.wait_ge(const_in, 16)
            dve.tensor_copy(ident_bf[:], const[:, C_ID:C_DELTA]).then_inc(ident_ready, 1)
            dve.wait_ge(xrest_in, 16)
            norm_stats(1, range(NT, 2 * NT))
            dve.wait_ge(bvr_in, 16)
            dve.wait_ge(rowb_c, 1)
            evacuate_rows(0)
            rank_top(0)
            one_hot(0)
            norm_stats(2, range(2 * NT, NG * NT))
            hidden_lo(0, 0)
            hidden_lo(0, 1)
            mask_scores(0)
            dve.wait_ge(rstd_ready, 3)
            dve.wait_ge(xT_in, 16)
            with dve.Fori(0, NG - 1) as g:
                n = g + 1
                hidden_lo(g, 2)
                norm_apply(n)
                hidden_lo(g, 3)
                hidden_lo(g, 4)
                split_x(n)
                add_attention(g)
                evacuate_rows(n)
                rank_top(n)
                hidden_lo(g, 5)
                one_hot(n)
                hidden_lo(g, 6)
                hidden_lo(g, 7)
                hidden_lo(n, 0)
                combine(g)
                hidden_lo(n, 1)
                mask_scores(n)
            for b in range(2, NB):
                hidden_lo(NG - 1, b)
                if b == 4:
                    add_attention(NG - 1)
            combine(NG - 1)

        @block.tensor
        def _(pe):
            ident = const[:, C_ID:C_DELTA]

            def hidden_products(g, b):
                w = slice(b * P, (b + 1) * P)
                acc = ps_hid[b % RP][:]
                wait(pe, hid_lo_ready, g * NB + b + 1)
                wait(pe, xT_lo_ready, g + 1)
                pe.matmul(acc, w1_hi[:, w], cols(xT_hi, g), start=True, stop=False)
                pe.matmul(acc, w1_hi[:, w], cols(xT_lo, g), start=False, stop=False)
                pe.matmul(acc, w1_lo[:, w], cols(xT_hi, g), start=False, stop=False)

            def hidden_mask(g, b):
                wait(pe, route_ready, g + 1)
                pe.matmul(ps_hid[b % RP][:], mask_w[:, b * EB:(b + 1) * EB, :], cols(route, g),
                          start=False, stop=True).then_inc(hid_mm, 1)

            def hidden(g, b):
                hidden_products(g, b)
                hidden_mask(g, b)

            def output(g, b):
                w = slice(b * D, (b + 1) * D)
                wait(pe, hid_lo_ready, g * NB + b + 1 + RP)
                if b == 0:
                    wait(pe, out_ready, g + 1)
                if b == NB - 1:
                    pe.matmul(ps_y[:], b_rows[:, H:], cols(route, g), start=False, stop=False)
                pe.matmul(ps_y[:], w2_hi[:, w], hid_hi[:, b % RH, :], start=b == 0, stop=False)
                pe.matmul(ps_y[:], w2_lo[:, w], hid_hi[:, b % RH, :], start=False, stop=False)
                last = pe.matmul(ps_y[:], w2_hi[:, w], hid_lo[:, b % RH, :], start=False, stop=b == NB - 1)
                last.then_inc(hid_used, 1)

            def transpose_x(n):
                wait(pe, key_hi_ready, n)
                for t in range(NT):
                    wait(pe, xn_ready, NT * n + t + 1)
                    last = pe.transpose(ps_xk[:, t * P:(t + 1) * P], xn[:, t, :], ident)
                last.then_inc(xT_mm, 1)

            def row_products(n):
                wait(pe, xT_ready, n + 1)
                wait(pe, sc_ready, n)
                for t in range(NT):
                    bank = (ps_a, ps_b)[t // 2]
                    last = pe.matmul(bank[:, (t % 2) * SEQ:(t % 2) * SEQ + VW], xT[:, t, :], row_w[:],
                                     start=True, stop=True)
                last.then_inc(rows_mm, 1)

            def key_products(n):
                wait(pe, xT_lo_ready, n + 1)
                wait(pe, xT_ready, n + 1)
                pe.matmul(ps_xk[:], g_hi[:], cols(xT_hi, n), start=True, stop=False)
                pe.matmul(ps_xk[:], g_hi[:], cols(xT_lo, n), start=False, stop=False)
                pe.matmul(ps_xk[:], g_lo[:], cols(xT_hi, n), start=False, stop=True).then_inc(key_mm, 1)

            def transpose_route(n):
                wait(pe, onehot_ready, n + 1)
                wait(pe, route_ready, n)
                for t in range(NT):
                    last = pe.transpose(ps_route[:, t * (P // 2):(t + 1) * (P // 2)].bitcast(BF16),
                                        onehot[:, t].rearrange("p q e -> p (q e)"), ident_bf[:])
                last.then_inc(route_mm, 1)

            def score_products(n):
                wait(pe, key_lo_ready, n + 1)
                wait(pe, rows_ready, 2 * n + 2)
                for s in range(NS):
                    xs_hi = xT_hi[:, bass.ds(n * GT + s * SEQ, SEQ)]
                    xs_lo = xT_lo[:, bass.ds(n * GT + s * SEQ, SEQ)]
                    acc = ps_a[:, s * SEQ:(s + 1) * SEQ]
                    pe.matmul(acc, keyT_hi[:, s, :], xs_hi, start=True, stop=False)
                    pe.matmul(acc, keyT_hi[:, s, :], xs_lo, start=False, stop=False)
                    pe.matmul(acc, keyT_lo[:, s, :], xs_hi, start=False, stop=True)
                for s in range(NS):
                    last = pe.matmul(ps_b[:, s * P:(s + 1) * P], keyT[:, 2 * s + 1, :], xT[:, 2 * s + 1, :],
                                     start=True, stop=True)
                last.then_inc(sc_mm, 1)

            def attention_products(n):
                wait(pe, sc_lo_ready, n + 1)
                wait(pe, v_lo_ready, n + 1)
                wait(pe, att_ready, n)
                for s in range(NS):
                    acc = ps_att[:, s * SEQ:(s + 1) * SEQ]
                    pe.matmul(acc, v_hi[:, s, :], sc0_hi[:, s, :], start=True, stop=False)
                    pe.matmul(acc, v_hi[:, s, :], sc0_lo[:, s, :], start=False, stop=False)
                    pe.matmul(acc, v_lo[:, s, :], sc0_hi[:, s, :], start=False, stop=False)
                    last = pe.matmul(ps_att[:, s * SEQ + P:(s + 1) * SEQ], rows[:, 2 * s + 1, 0:D], sc1[:, s, :],
                                     start=False, stop=True)
                last.then_inc(att_mm, 1)

            pe.wait_ge(wattn_in, 16)
            wq, wk = wattn[:, A_Q:A_K], wattn[:, A_K:A_V]
            pe.matmul(ps_route[:, 0:D], wk, wq, start=True, stop=True)
            pe.matmul(ps_route[:, D:D + 1], wq, wattn[:, A_BK:A_W], start=True, stop=True)
            pe.matmul(ps_route[:, D + 1:D + 2], wk, wattn[:, A_BQ:A_BK], start=True, stop=True)
            pe.wait_ge(bqk_ready, 1)
            pe.wait_ge(ones_ready, 1)
            pe.matmul(ps_route[:, D + 2:D + 3], ones[:], bqk[:], start=True, stop=True).then_inc(setup_mm, 1)
            pe.sem_inc(hid_used, RH)
            pe.wait_ge(const_in, 16)
            transpose_x(0)
            pe.wait_ge(roww_ready, 2)
            row_products(0)
            pe.wait_ge(g_lo_ready, 1)
            key_products(0)
            pe.wait_ge(w1_first_ready, 1)
            hidden_products(0, 0)
            hidden_products(0, 1)
            pe.wait_ge(ident_ready, 1)
            transpose_route(0)
            score_products(0)
            pe.wait_ge(mask_ready, 1)
            hidden_mask(0, 0)
            hidden_mask(0, 1)
            pe.wait_ge(w1_lo_ready, 1)
            pe.wait_ge(w2_lo_ready, 1)
            with pe.Fori(0, NG - 1) as g:
                n = g + 1
                hidden(g, 2)
                output(g, 0)
                hidden(g, 3)
                output(g, 1)
                hidden(g, 4)
                transpose_x(n)
                output(g, 2)
                attention_products(g)
                row_products(n)
                hidden(g, 5)
                key_products(n)
                output(g, 3)
                hidden(g, 6)
                output(g, 4)
                hidden(g, 7)
                output(g, 5)
                transpose_route(n)
                output(g, 6)
                hidden(n, 0)
                output(g, 7)
                hidden(n, 1)
                score_products(n)
            for b in range(2, NB):
                hidden(NG - 1, b)
                output(NG - 1, b - 2)
                if b == 4:
                    attention_products(NG - 1)
            output(NG - 1, NB - 2)
            output(NG - 1, NB - 1)


def kernel(L0_attn_x, L0_attn_W_qkv, L0_attn_b_qkv, L0_ffn_router_w, L0_ffn_router_b,
           L0_ffn_weights1, L0_ffn_bias1, L0_ffn_weights2, L0_ffn_bias2):
    import concourse.bacc as bacc
    from concourse.bass_utils import run_bass_kernel_spmd

    xs, w, b = np.asarray(L0_attn_x), np.asarray(L0_attn_W_qkv), np.asarray(L0_attn_b_qkv)
    mask_row = np.zeros((E, H + D), np.float32)
    mask_row[:, 0:H] = BIG
    wq, wk, wv = w[0:D], w[D:2 * D], w[2 * D:]
    data = {
        "in_x": xs.reshape(TOK // P, P, D).transpose(1, 0, 2).reshape(P, TOK),
        "in_xT": xs.reshape(TOK, D).T,
        "in_wattn": np.concatenate([wq, wk, wv.T, np.asarray(L0_ffn_router_w).T,
                                    b[0:D, None], b[D:2 * D, None]], axis=1),
        "in_bvr": np.concatenate([b[2 * D:], np.asarray(L0_ffn_router_b)]),
        "in_w1": np.asarray(L0_ffn_weights1).transpose(1, 0, 2).reshape(D, E * H),
        "in_w2": np.asarray(L0_ffn_weights2).reshape(NB, P, D).transpose(1, 0, 2).reshape(P, NB * D),
        "in_b12": np.concatenate([mask_row] + 3 * [np.concatenate([np.asarray(L0_ffn_bias1),
                                                                   np.asarray(L0_ffn_bias2)], axis=1)]),
        "in_const": shape_constants(),
    }
    data = {k: np.ascontiguousarray(v) for k, v in data.items()}
    nc = bacc.Bacc("TRN2", target_bir_lowering=False, num_devices=1)
    aps = [nc.dram_tensor(k, v.shape, mybir.dt.from_np(v.dtype), kind="ExternalInput").ap()
           for k, v in data.items()]
    out = nc.dram_tensor("outT_d", (P, TOK), F32, kind="ExternalOutput").ap()
    build(nc, *aps, out)
    got = run_bass_kernel_spmd(nc, [data], core_ids=[0]).results[0]["outT_d"]
    return got.T.reshape(BATCH, SEQ, D)
```

```python
from contextlib import ExitStack

import numpy as np

import concourse.bass as bass
from concourse import mybir

F32 = mybir.dt.float32
F32R = mybir.dt.float32r
BF16 = mybir.dt.bfloat16
ALU = mybir.AluOpType
ACT = mybir.ActivationFunctionType
AX = mybir.AxisListType

P = 128
D = 128
SEQ = 256
BATCH = 8
TOK = BATCH * SEQ
GT = 512
NG = TOK // GT
NT = GT // P
NS = GT // SEQ
E = 32
H = 32
EB = P // H
NB = E // EB
VW = D + E + 1
ALPHA = 0.99
EPS = 1e-5
LEAD = 4
TAIL = 5
WARM = 8
W1_FIRST = 2 * P
W2_FIRST = NB // 2 * D

C_ID = 0
C_DESC = C_ID + P
C_EXPERT = C_DESC + E
C_MASK = C_EXPERT + NB
C_W = C_MASK + SEQ

A_Q = 0
A_BQ = A_Q + D
A_BK = A_BQ + 1
A_K = A_BK + 1
A_V = A_K + D
A_R = A_V + D
A_W = A_R + E

S_G = 0
S_W = S_G + D
S_U = S_W + 1
S_C = S_U + 1 + D


def shape_constants():
    c = np.zeros((P, C_W), np.float32)
    j, i = np.arange(P)[:, None], np.arange(SEQ)[None, :]
    decay = np.float32(ALPHA) ** np.maximum(i - j, 0).astype(np.float32)
    c[:, C_MASK:C_W] = np.where(i >= j, decay / np.float32(np.sqrt(D)), 0)
    c[:, C_ID:C_DESC] = np.eye(P)
    c[:, C_DESC:C_EXPERT] = E - np.arange(E)
    c[:, C_EXPERT:C_MASK] = E - (EB * np.arange(NB)[None, :] + np.arange(P)[:, None] // H)
    return c


def wait(eng, sem, value):
    if isinstance(value, int) and value <= 0:
        return
    eng.wait_ge(sem, value)


def build(nc, x_d, xT_d, wattn_d, bvr_d, w1_d, w2_d, b1_d, b2_d, const_d, out_d):
    with ExitStack() as ctx:
        def sb(name, shape, dt=F32):
            return ctx.enter_context(nc.sbuf_tensor(name, shape, dt))

        def ps(name, shape=(P, GT), dt=F32):
            return ctx.enter_context(nc.psum_tensor(name, list(shape), dt))

        def sem(name):
            return ctx.enter_context(nc.semaphore(name))

        const = sb("const", [P, C_W])
        ident_bf = sb("ident_bf", [P, P], BF16)
        wattn = sb("wattn", [P, A_W])
        w1 = sb("w1", [P, E * H])
        w1_hi = sb("w1_hi", [P, E * H], F32R)
        w1_lo = sb("w1_lo", [P, E * H], F32R)
        w2 = sb("w2", [P, NB * D])
        w2_hi = sb("w2_hi", [P, NB * D], F32R)
        w2_lo = sb("w2_lo", [P, NB * D], F32R)
        row_w = sb("row_w", [P, VW])
        row_b = sb("row_b", [P, VW])
        g_hi = sb("g_hi", [P, D], F32R)
        g_lo = sb("g_lo", [P, D], F32R)
        u_col = sb("u_col", [P, 1])
        bqk = sb("bqk", [P, 1])
        ones = sb("ones", [P, P])
        minus_half = sb("minus_half", [P, NT])
        warm = sb("warm", [P, 1])
        b1_col = sb("b1_col", [P, NB])
        b2 = sb("b2", [P, D])
        b2_rest = sb("b2_rest", [P, D])
        b2_rest2 = sb("b2_rest2", [P, D])
        b2_parts = sb("b2_parts", [P, D], BF16)
        x = sb("x", [P, TOK])
        xT_hi = sb("xT_hi", [P, TOK], F32R)
        xT_lo = sb("xT_lo", [P, TOK], F32R)
        route = sb("route", [P, TOK], BF16)
        index = sb("index", [P, TOK], BF16)
        x_byT = sb("x_byT", [P, TOK])
        attT = sb("attT", [P, TOK])
        outT = sb("outT", [P, TOK])
        stats = sb("stats", [P, NT, 6])
        mv = sb("mv", [P, NT, 2])
        var_eps = sb("var_eps", [P, NT])
        rstd = sb("rstd", [P, NT])
        xn = sb("xn", [P, NT, D])
        xT = sb("xT", [P, NT, P])
        v = sb("v", [P, NT, D])
        route_rows = sb("route_rows", [P, NT, E + 1])
        v_hi = sb("v_hi", [P, NS, D], F32R)
        v_lo = sb("v_lo", [P, NS, D], F32R)
        keyT = sb("keyT", [P, NT, P])
        keyT_hi = sb("keyT_hi", [P, NS, P], F32R)
        keyT_lo = sb("keyT_lo", [P, NS, P], F32R)
        top = sb("top", [P, NT])
        is_top = sb("is_top", [P, NT, E])
        rank = sb("rank", [P, NT, E])
        top_rank = sb("top_rank", [P, NT])
        onehot = sb("onehot", [P, NT, 4, E], BF16)
        rank_rows = sb("rank_rows", [P, NT, P], BF16)
        sc0 = sb("sc0", [P, NS, SEQ])
        sc0_hi = sb("sc0_hi", [P, NS, SEQ], F32R)
        sc0_lo = sb("sc0_lo", [P, NS, SEQ], F32R)
        sc1 = sb("sc1", [P, NS, P])
        RH = NB
        hid = sb("hid", [P, RH, GT])
        routed = sb("routed", [P, RH, GT])
        hid_hi = sb("hid_hi", [P, RH, GT], F32R)
        hid_lo = sb("hid_lo", [P, RH, GT], F32R)

        RP = 2
        ps_hid = [ps(f"ps_hid{i}") for i in range(RP)]
        ps_y = ps("ps_y")
        ps_xk = ps("ps_xk")
        ps_a = ps("ps_a")
        ps_b = ps("ps_b")
        ps_att = ps("ps_att")
        ps_route = ps("ps_route")

        x0_in, xrest_in, xT_in = [sem(name) for name in ("x0_in", "xrest_in", "xT_in")]
        wattn_in, wvr_in, bvr_in = [sem(name) for name in ("wattn_in", "wvr_in", "bvr_in")]
        w1_in, w2_in, b1_in, b2_in = [sem(name) for name in ("w1_in", "w2_in", "b1_in", "b2_in")]
        const_in, mask_in = [sem(name) for name in ("const_in", "mask_in")]
        ones_ready, half_set, bqk_ready, setup_mm, rowb_ready = [
            sem(name) for name in ("ones_ready", "half_set", "bqk_ready", "setup_mm", "rowb_ready")]
        g_hi_ready, g_lo_ready, roww_ready, u_ready, ident_ready = [
            sem(name) for name in ("g_hi_ready", "g_lo_ready", "roww_ready", "u_ready", "ident_ready")]
        w1_hi_ready, w1_first_ready, w1_lo_ready = [
            sem(name) for name in ("w1_hi_ready", "w1_first_ready", "w1_lo_ready")]
        w2_hi_ready, w2_first_ready, w2_lo_ready = [
            sem(name) for name in ("w2_hi_ready", "w2_first_ready", "w2_lo_ready")]
        b2_split = sem("b2_split")
        stats_step = sem("stats_step")
        eps_ready = sem("eps_ready")
        rstd_ready = sem("rstd_ready")
        xn_ready = sem("xn_ready")
        xT_mm = sem("xT_mm")
        xT_ready = sem("xT_ready")
        xT_hi_ready = sem("xT_hi_ready")
        xT_lo_ready = sem("xT_lo_ready")
        rows_mm = sem("rows_mm")
        route_rows_ready = sem("route_rows_ready")
        v_ready = sem("v_ready")
        v_hi_ready = sem("v_hi_ready")
        v_lo_ready = sem("v_lo_ready")
        key_mm = sem("key_mm")
        key_ready = sem("key_ready")
        key_hi_ready = sem("key_hi_ready")
        key_lo_ready = sem("key_lo_ready")
        argmax_step = sem("argmax_step")
        onehot_ready = sem("onehot_ready")
        rank_rows_ready = sem("rank_rows_ready")
        route_mm = sem("route_mm")
        route_ready = sem("route_ready")
        index_mm = sem("index_mm")
        index_ready = sem("index_ready")
        sc_mm = sem("sc_mm")
        sc_ready = sem("sc_ready")
        sc_hi_ready = sem("sc_hi_ready")
        sc_lo_ready = sem("sc_lo_ready")
        att_mm = sem("att_mm")
        att_ready = sem("att_ready")
        out_ready = sem("out_ready")
        half_mm = sem("half_mm")
        half_ready = sem("half_ready")
        out_stored = sem("out_stored")
        hid_mm = sem("hid_mm")
        hid_ready = sem("hid_ready")
        routed_ready = sem("routed_ready")
        hid_hi_ready = sem("hid_hi_ready")
        hid_lo_ready = sem("hid_lo_ready")
        tail_lo_ready = sem("tail_lo_ready")
        hid_used = sem("hid_used")

        def cols(t, n):
            return t[:, bass.ts(n, GT)]

        def half(t, h):
            return t[:, (NG - 1) * GT + h * GT // 2:(NG - 1) * GT + (h + 1) * GT // 2]

        def last_y(h):
            return (ps_y, ps_xk)[h][:, 0:GT // 2]

        block = ctx.enter_context(nc.Block())

        @block.sync
        def _(sp):
            sp.dma_start(x[:, 0:GT], x_d[:, 0:GT]).then_inc(x0_in, 16)
            sp.dma_start(const[:, 0:C_MASK], const_d[:, 0:C_MASK]).then_inc(const_in, 16)
            sp.dma_start(w1[:], w1_d).then_inc(w1_in, 16)
            sp.dma_start(w2[:], w2_d).then_inc(w2_in, 16)
            sp.dma_start(b1_col[:], b1_d).then_inc(b1_in, 16)
            sp.dma_start(b2[:], b2_d).then_inc(b2_in, 16)
            sp.dma_start(x[:, GT:], x_d[:, GT:]).then_inc(xrest_in, 16)
            sp.dma_start(const[:, C_MASK:], const_d[:, C_MASK:]).then_inc(mask_in, 16)
            sp.dma_start(x_byT[:], xT_d).then_inc(xT_in, 16)
            with sp.Fori(0, NG - 1) as n:
                sp.wait_ge(out_ready, n + 2)
                sp.dma_start(cols(out_d, n), cols(outT, n)).then_inc(out_stored, 16)
            for h in range(2):
                sp.wait_ge(half_ready, h + 1)
                sp.dma_start(half(out_d, h), half(outT, h)).then_inc(out_stored, 16)
            sp.wait_ge(out_stored, 16 * (NG + 1))

        @block.gpsimd
        def _(pool):
            pool.memset(ones[:], 1.0).then_inc(ones_ready, 1)
            pool.memset(minus_half[:], -0.5).then_inc(half_set, 1)
            pool.dma_start(row_b[:, 0:D + E], bvr_d.partition_broadcast(P)).then_inc(bvr_in, 16)

            def hidden_lo(g, b):
                wait(pool, hid_hi_ready, g * NB + b + 1)
                pool.tensor_tensor(hid_lo[:, b % RH, :], routed[:, b % RH, :], hid_hi[:, b % RH, :].bitcast(F32),
                                   ALU.subtract).then_inc(hid_lo_ready, 1)

            def norm_scale(n):
                wait(pool, eps_ready, n + 1)
                pool.tensor_tensor(rstd[:], var_eps[:], minus_half[:], ALU.pow).then_inc(rstd_ready, 1)

            def split_values(n):
                wait(pool, v_hi_ready, n + 1)
                wait(pool, att_mm, n)
                pool.tensor_tensor(v_lo[:], v[:, 0:NT:2, :], v_hi[:].bitcast(F32),
                                   ALU.subtract).then_inc(v_lo_ready, 1)

            def split_keys(n):
                wait(pool, key_hi_ready, n + 1)
                wait(pool, sc_mm, n)
                pool.tensor_tensor(keyT_lo[:], keyT[:, 0:NT:2, :], keyT_hi[:].bitcast(F32),
                                   ALU.subtract).then_inc(key_lo_ready, 1)

            def split_scores(n):
                wait(pool, sc_hi_ready, n + 1)
                wait(pool, att_mm, n)
                pool.tensor_tensor(sc0_lo[:], sc0[:], sc0_hi[:].bitcast(F32),
                                   ALU.subtract).then_inc(sc_lo_ready, 1)

            pool.sem_inc(hid_lo_ready, RH)
            pool.wait_ge(half_set, 1)
            norm_scale(0)
            pool.wait_ge(b2_split, 1)
            pool.tensor_tensor(b2_rest[:], b2[:], b2_parts[:], ALU.subtract).then_inc(b2_split, 1)
            pool.wait_ge(w1_hi_ready, 2)
            pool.tensor_tensor(w1_lo[:, W1_FIRST:], w1[:, W1_FIRST:], w1_hi[:, W1_FIRST:].bitcast(F32),
                               ALU.subtract).then_inc(w1_lo_ready, 1)
            pool.wait_ge(b2_split, 3)
            pool.tensor_tensor(b2_rest2[:], b2_rest[:], b2_parts[:], ALU.subtract).then_inc(b2_split, 1)
            split_keys(0)
            pool.wait_ge(w2_hi_ready, 1)
            pool.tensor_tensor(w2_lo[:, W2_FIRST:], w2[:, W2_FIRST:], w2_hi[:, W2_FIRST:].bitcast(F32),
                               ALU.subtract).then_inc(w2_lo_ready, 1)
            split_values(0)
            hidden_lo(0, 0)
            hidden_lo(0, 1)
            with pool.Fori(0, NG - 1) as g:
                n = g + 1
                norm_scale(n)
                hidden_lo(g, 2)
                split_scores(g)
                hidden_lo(g, 3)
                hidden_lo(g, 4)
                hidden_lo(g, 5)
                split_keys(n)
                hidden_lo(g, 6)
                hidden_lo(g, 7)
                split_values(n)
                hidden_lo(n, 0)
                hidden_lo(n, 1)
            hidden_lo(NG - 1, 2)
            split_scores(NG - 1)
            for b in range(LEAD - 1, TAIL):
                hidden_lo(NG - 1, b)

        @block.scalar
        def _(act):
            act.dma_start(wattn[:, 0:A_V], wattn_d[:, 0:A_V]).then_inc(wattn_in, 16)
            act.dma_start(wattn[:, A_V:], wattn_d[:, A_V:]).then_inc(wvr_in, 16)

            def hidden_relu(g, b):
                wait(act, hid_mm, g * NB + b + 1)
                wait(act, routed_ready, g * NB + b + 1)
                act.activation(hid[:, b % RH, :], ps_hid[b % RP][:], ACT.Relu,
                               bias=b1_col[:, b:b + 1]).then_inc(hid_ready, 1)

            def hidden_hi(g, b):
                wait(act, routed_ready, g * NB + b + 1 + RH)
                wait(act, hid_used, g * NB + b + 1)
                act.activation(hid_hi[:, b % RH, :], routed[:, b % RH, :], ACT.Copy).then_inc(hid_hi_ready, 1)

            def evacuate_x(n):
                wait(act, xT_mm, n + 1)
                wait(act, sc_mm, n)
                act.activation(xT[:], ps_xk[:], ACT.Copy).then_inc(xT_ready, 1)
                act.activation(cols(xT_hi, n), ps_xk[:], ACT.Copy).then_inc(xT_hi_ready, 1)

            def value_hi(n):
                wait(act, v_ready, 2 * n + 2)
                wait(act, att_mm, n)
                act.activation(v_hi[:], v[:, 0:NT:2, :], ACT.Copy).then_inc(v_hi_ready, 1)

            def evacuate_keys(n):
                wait(act, key_mm, n + 1)
                wait(act, sc_mm, n)
                wait(act, key_lo_ready, n)
                if isinstance(n, int) and n == 0:
                    act.wait_ge(u_ready, 1)
                act.activation(keyT[:], ps_xk[:], ACT.Identity, bias=u_col[:]).then_inc(key_ready, 1)
                act.activation(keyT_hi[:], ps_xk[:].rearrange("p (t k) -> p t k", t=NT)[:, 0:NT:2, :],
                               ACT.Identity, bias=u_col[:]).then_inc(key_hi_ready, 1)

            def evacuate_route(n):
                wait(act, route_mm, n + 1)
                act.activation(cols(route, n), ps_route[:, 0:GT // 2].bitcast(BF16), ACT.Copy).then_inc(route_ready, 1)

            def evacuate_index(n):
                wait(act, index_mm, n + 1)
                act.activation(cols(index, n), ps_route[:], ACT.Copy).then_inc(index_ready, 1)

            def scores_hi(n):
                wait(act, sc_ready, n + 1)
                wait(act, att_mm, n)
                act.activation(sc0_hi[:], sc0[:], ACT.Copy).then_inc(sc_hi_ready, 1)

            act.wait_ge(ones_ready, 1)
            act.activation(warm[:], ones[:, 0:1], ACT.Relu)
            act.sem_inc(hid_ready, RP)
            act.wait_ge(setup_mm, 1)
            act.activation(u_col[:], ps_route[:, S_U:S_U + 1], ACT.Copy).then_inc(u_ready, 1)
            act.activation(row_w[:, D + E:VW], ps_route[:, S_W:S_U], ACT.Copy).then_inc(roww_ready, 1)
            act.wait_ge(wvr_in, 16)
            act.activation(row_w[:, 0:D + E], wattn[:, A_V:A_W], ACT.Copy).then_inc(roww_ready, 1)
            act.activation(row_b[:, D + E:VW], ps_route[:, S_C:S_C + 1], ACT.Copy).then_inc(rowb_ready, 1)
            act.activation(g_hi[:], ps_route[:, 0:D], ACT.Copy).then_inc(g_hi_ready, 1)
            act.wait_ge(w1_in, 16)
            act.activation(w1_hi[:, 0:W1_FIRST], w1[:, 0:W1_FIRST], ACT.Copy).then_inc(w1_hi_ready, 1)
            evacuate_x(0)
            act.activation(w1_hi[:, W1_FIRST:], w1[:, W1_FIRST:], ACT.Copy).then_inc(w1_hi_ready, 1)
            act.wait_ge(b2_in, 16)
            act.activation(b2_parts[:], b2[:], ACT.Copy).then_inc(b2_split, 1)
            act.wait_ge(w2_in, 16)
            act.activation(w2_hi[:], w2[:], ACT.Copy).then_inc(w2_hi_ready, 1)
            evacuate_keys(0)
            act.wait_ge(b2_split, 2)
            act.activation(b2_parts[2 * E:, :], b2_rest[2 * E:, :], ACT.Copy).then_inc(b2_split, 1)
            act.wait_ge(b1_in, 16)
            hidden_relu(0, 0)
            hidden_relu(0, 1)
            evacuate_index(0)
            value_hi(0)
            hidden_relu(0, 2)
            hidden_hi(0, 0)
            act.wait_ge(b2_split, 4)
            act.activation(b2_parts[3 * E:, :], b2_rest2[3 * E:, :], ACT.Copy).then_inc(b2_split, 1)
            evacuate_route(0)
            hidden_hi(0, 1)
            hidden_relu(0, 3)
            hidden_hi(0, 2)
            with act.Fori(0, NG - 1) as g:
                n = g + 1
                hidden_relu(g, 4)
                hidden_relu(g, 5)
                scores_hi(g)
                hidden_relu(g, 6)
                evacuate_x(n)
                hidden_hi(g, 3)
                hidden_relu(g, 7)
                hidden_hi(g, 4)
                hidden_hi(g, 5)
                evacuate_keys(n)
                hidden_hi(g, 6)
                evacuate_index(n)
                hidden_relu(n, 0)
                hidden_hi(g, 7)
                hidden_relu(n, 1)
                value_hi(n)
                hidden_relu(n, 2)
                hidden_hi(n, 0)
                evacuate_route(n)
                hidden_hi(n, 1)
                hidden_relu(n, 3)
                hidden_hi(n, 2)
            hidden_relu(NG - 1, 4)
            hidden_relu(NG - 1, 5)
            scores_hi(NG - 1)
            hidden_hi(NG - 1, 3)
            hidden_relu(NG - 1, 6)
            hidden_hi(NG - 1, 4)
            hidden_relu(NG - 1, 7)
            for b in range(5, NB):
                hidden_hi(NG - 1, b)

        @block.vector
        def _(dve):
            def hidden_routed(g, b):
                wait(dve, hid_ready, g * NB + b + 1 + RP)
                wait(dve, hid_lo_ready, g * NB + b + 1)
                dve.scalar_tensor_tensor(routed[:, b % RH, :], cols(index, g),
                                         const[:, C_EXPERT + b:C_EXPERT + b + 1], hid[:, b % RH, :],
                                         ALU.is_equal, ALU.mult).then_inc(routed_ready, 1)

            def tail_lo(b):
                dve.wait_ge(hid_hi_ready, (NG - 1) * NB + b + 1)
                dve.tensor_tensor(hid_lo[:, b % RH, :], routed[:, b % RH, :], hid_hi[:, b % RH, :].bitcast(F32),
                                  ALU.subtract).then_inc(tail_lo_ready, 1)

            def norm_stats(n):
                for t in range(NT):
                    last = dve.bn_stats(stats[:, t, :], x[:, bass.ds(n * GT + t * P, P)])
                last.then_inc(stats_step, 1)
                wait(dve, stats_step, 2 * n + 1)
                if not isinstance(n, int):
                    dve.nop(nofuse=True)
                for t in range(NT):
                    last = dve.bn_aggr(mv[:, t, :], stats[:, t, :])
                last.then_inc(stats_step, 1)
                wait(dve, stats_step, 2 * n + 2)
                dve.tensor_scalar(var_eps[:], mv[:, :, 1], EPS, None, ALU.add).then_inc(eps_ready, 1)

            def norm_apply(n):
                wait(dve, rstd_ready, n + 1)
                wait(dve, xT_mm, n)
                for t in range(NT):
                    dve.tensor_scalar(xn[:, t, :], x[:, bass.ds(n * GT + t * P, P)],
                                      mv[:, t, 0:1], rstd[:, t:t + 1], ALU.subtract,
                                      ALU.mult).then_inc(xn_ready, 1)

            def split_x(n):
                wait(dve, xT_hi_ready, n + 1)
                dve.tensor_tensor(cols(xT_lo, n), ps_xk[:], cols(xT_hi, n).bitcast(F32),
                                  ALU.subtract).then_inc(xT_lo_ready, 1)

            def evacuate_route_rows(n):
                wait(dve, rows_mm, n + 1)
                for k, bank in enumerate((ps_a, ps_b)):
                    dve.tensor_tensor(route_rows[:, 2 * k:2 * k + 2, :],
                                      bank[:].rearrange("p (t c) -> p t c", t=2)[:, :, D:VW],
                                      row_b[:, D:VW].unsqueeze(1).broadcast_to([P, 2, E + 1]),
                                      ALU.add).then_inc(route_rows_ready, 1)

            def evacuate_values(n):
                wait(dve, rows_mm, n + 1)
                wait(dve, att_mm, n)
                wait(dve, v_lo_ready, n)
                for k, bank in enumerate((ps_a, ps_b)):
                    dve.tensor_tensor(v[:, 2 * k:2 * k + 2, :],
                                      bank[:].rearrange("p (t c) -> p t c", t=2)[:, :, 0:D],
                                      row_b[:, 0:D].unsqueeze(1).broadcast_to([P, 2, D]),
                                      ALU.add).then_inc(v_ready, 1)

            def rank_top(n):
                logits = route_rows[:, :, 0:E]
                wait(dve, route_rows_ready, 2 * n + 2)
                dve.tensor_reduce(top[:], logits, AX.X, ALU.max).then_inc(argmax_step, 1)
                wait(dve, argmax_step, 5 * n + 1)
                dve.tensor_tensor(is_top[:], logits, top[:].unsqueeze(2).broadcast_to([P, NT, E]),
                                  ALU.is_equal).then_inc(argmax_step, 1)
                wait(dve, argmax_step, 5 * n + 2)
                dve.tensor_tensor(rank[:], is_top[:],
                                  const[:, C_DESC:C_EXPERT].unsqueeze(1).broadcast_to([P, NT, E]),
                                  ALU.mult).then_inc(argmax_step, 1)

            def spread_rank(n):
                wait(dve, argmax_step, 5 * n + 3)
                dve.tensor_reduce(top_rank[:], rank[:], AX.X, ALU.max).then_inc(argmax_step, 1)
                wait(dve, argmax_step, 5 * n + 4)
                wait(dve, index_mm, n)
                dve.tensor_copy(rank_rows[:], top_rank[:].unsqueeze(2).broadcast_to([P, NT, P]))\
                   .then_inc(rank_rows_ready, 1)

            def one_hot(n):
                wait(dve, route_mm, n)
                dve.tensor_tensor(onehot[:, :, 0, :], rank[:], top_rank[:].unsqueeze(2).broadcast_to([P, NT, E]),
                                  ALU.is_equal).then_inc(argmax_step, 1)
                wait(dve, argmax_step, 5 * n + 5)
                dve.tensor_copy(onehot[:, :, 1:4, :], onehot[:, :, 0:1, :].broadcast_to([P, NT, 3, E]))\
                   .then_inc(onehot_ready, 1)

            def mask_scores(n):
                wait(dve, sc_mm, n + 1)
                wait(dve, att_mm, n)
                wait(dve, sc_lo_ready, n)
                for s in range(NS):
                    dve.scalar_tensor_tensor(sc0[:, s, :], ps_a[:, s * SEQ:(s + 1) * SEQ],
                                             route_rows[:, 2 * s, E:], const[:, C_MASK:C_MASK + SEQ],
                                             ALU.add, ALU.mult)
                for s in range(NS):
                    last = dve.scalar_tensor_tensor(sc1[:, s, :], ps_b[:, s * P:(s + 1) * P],
                                                    route_rows[:, 2 * s + 1, E:], const[:, C_MASK:C_MASK + P],
                                                    ALU.add, ALU.mult)
                last.then_inc(sc_ready, 1)

            def add_attention(n):
                wait(dve, att_mm, n + 1)
                dve.tensor_tensor(cols(attT, n), ps_att[:], cols(x_byT, n), ALU.add).then_inc(att_ready, 1)

            def combine(g):
                wait(dve, att_ready, g + 1)
                wait(dve, hid_used, RH + NB * (g + 1))
                dve.scalar_tensor_tensor(cols(outT, g), ps_y[:], 0.0, cols(attT, g), ALU.max,
                                         ALU.add).then_inc(out_ready, 1)

            def combine_half(h):
                if h == 0:
                    wait(dve, att_ready, NG)
                wait(dve, half_mm, h + 1)
                dve.scalar_tensor_tensor(half(outT, h), last_y(h), 0.0, half(attT, h), ALU.max,
                                         ALU.add).then_inc(half_ready, 1)

            dve.sem_inc(routed_ready, RH)
            dve.sem_inc(out_ready, 1)
            dve.wait_ge(x0_in, 16)
            norm_stats(0)
            dve.wait_ge(wattn_in, 16)
            dve.tensor_tensor(bqk[:], wattn[:, A_BQ:A_BK], wattn[:, A_BK:A_K], ALU.mult).then_inc(bqk_ready, 1)
            dve.wait_ge(const_in, 16)
            dve.tensor_copy(ident_bf[:], const[:, C_ID:C_DESC]).then_inc(ident_ready, 1)
            norm_apply(0)
            dve.wait_ge(g_hi_ready, 1)
            dve.tensor_tensor(g_lo[:], ps_route[:, 0:D], g_hi[:].bitcast(F32), ALU.subtract).then_inc(g_lo_ready, 1)
            dve.wait_ge(w1_hi_ready, 1)
            dve.tensor_tensor(w1_lo[:, 0:W1_FIRST], w1[:, 0:W1_FIRST], w1_hi[:, 0:W1_FIRST].bitcast(F32),
                              ALU.subtract).then_inc(w1_first_ready, 1)
            split_x(0)
            dve.wait_ge(bvr_in, 16)
            dve.wait_ge(rowb_ready, 1)
            evacuate_route_rows(0)
            rank_top(0)
            spread_rank(0)
            one_hot(0)
            evacuate_values(0)
            dve.wait_ge(index_ready, 1)
            hidden_routed(0, 0)
            dve.wait_ge(w2_hi_ready, 1)
            dve.tensor_tensor(w2_lo[:, 0:W2_FIRST], w2[:, 0:W2_FIRST], w2_hi[:, 0:W2_FIRST].bitcast(F32),
                              ALU.subtract).then_inc(w2_first_ready, 1)
            hidden_routed(0, 1)
            hidden_routed(0, 2)
            dve.wait_ge(xrest_in, 16)
            dve.wait_ge(mask_in, 16)
            dve.wait_ge(xT_in, 16)
            with dve.Fori(0, NG - 1) as g:
                n = g + 1
                norm_stats(n)
                mask_scores(g)
                norm_apply(n)
                hidden_routed(g, 3)
                hidden_routed(g, 4)
                hidden_routed(g, 5)
                split_x(n)
                evacuate_route_rows(n)
                rank_top(n)
                spread_rank(n)
                one_hot(n)
                hidden_routed(g, 6)
                evacuate_values(n)
                hidden_routed(g, 7)
                add_attention(g)
                dve.wait_ge(index_ready, n + 1)
                for b in range(LEAD - 1):
                    hidden_routed(n, b)
                combine(g)
            mask_scores(NG - 1)
            for b in range(LEAD - 1, NB):
                hidden_routed(NG - 1, b)
            for b in range(TAIL, NB):
                tail_lo(b)
            add_attention(NG - 1)
            combine_half(0)
            combine_half(1)

        @block.tensor
        def _(pe):
            ident = const[:, C_ID:C_DESC]

            def hidden(g, b):
                w = slice(b * P, (b + 1) * P)
                acc = ps_hid[b % RP][:]
                wait(pe, hid_ready, g * NB + b + 1)
                wait(pe, xT_lo_ready, g + 1)
                pe.matmul(acc, w1_hi[:, w], cols(xT_hi, g), start=True, stop=False)
                pe.matmul(acc, w1_hi[:, w], cols(xT_lo, g), start=False, stop=False)
                pe.matmul(acc, w1_lo[:, w], cols(xT_hi, g), start=False, stop=True).then_inc(hid_mm, 1)

            def output_hi(g, b):
                w = slice(b * D, (b + 1) * D)
                if b == 0:
                    wait(pe, out_ready, g + 1)
                    wait(pe, route_ready, g + 1)
                    pe.matmul(ps_y[:], b2_parts[:], cols(route, g), start=True, stop=False)
                wait(pe, hid_hi_ready, g * NB + b + 1)
                pe.matmul(ps_y[:], w2_hi[:, w], hid_hi[:, b % RH, :], start=False, stop=False)
                pe.matmul(ps_y[:], w2_lo[:, w], hid_hi[:, b % RH, :], start=False, stop=False)

            def output_lo(g, b):
                wait(pe, hid_lo_ready, g * NB + b + 1 + RH)
                pe.matmul(ps_y[:], w2_hi[:, b * D:(b + 1) * D], hid_lo[:, b % RH, :], start=False,
                          stop=b == NB - 1).then_inc(hid_used, 1)

            def output(g, b):
                output_hi(g, b)
                output_lo(g, b)

            def last_output(b):
                w = slice(b * D, (b + 1) * D)
                halves = [slice(h * GT // 2, (h + 1) * GT // 2) for h in range(2)]
                if b == 0:
                    wait(pe, out_ready, NG)
                    wait(pe, route_ready, NG)
                    wait(pe, key_hi_ready, NG)
                    for h in range(2):
                        pe.matmul(last_y(h), b2_parts[:], half(route, h), start=True, stop=False)
                wait(pe, hid_hi_ready, (NG - 1) * NB + b + 1)
                if b < NB - 1:
                    for h, half_cols in enumerate(halves):
                        pe.matmul(last_y(h), w2_hi[:, w], hid_hi[:, b, half_cols], start=False, stop=False)
                    for h, half_cols in enumerate(halves):
                        pe.matmul(last_y(h), w2_lo[:, w], hid_hi[:, b, half_cols], start=False, stop=False)
                if b >= TAIL:
                    wait(pe, tail_lo_ready, b - TAIL + 1)
                else:
                    wait(pe, hid_lo_ready, (NG - 1) * NB + b + 1 + RH)
                for h, half_cols in enumerate(halves):
                    if b == NB - 1:
                        pe.matmul(last_y(h), w2_hi[:, w], hid_hi[:, b, half_cols], start=False, stop=False)
                        pe.matmul(last_y(h), w2_lo[:, w], hid_hi[:, b, half_cols], start=False, stop=False)
                    product = pe.matmul(last_y(h), w2_hi[:, w], hid_lo[:, b, half_cols], start=False,
                                        stop=b == NB - 1)
                    if b == NB - 1:
                        product.then_inc(half_mm, 1)

            def transpose_x(n):
                wait(pe, key_hi_ready, n)
                for t in range(NT):
                    wait(pe, xn_ready, NT * n + t + 1)
                    last = pe.transpose(ps_xk[:, t * P:(t + 1) * P], xn[:, t, :], ident)
                last.then_inc(xT_mm, 1)

            def row_products(n):
                wait(pe, xT_ready, n + 1)
                wait(pe, sc_ready, n)
                for t in range(NT):
                    bank = (ps_a, ps_b)[t // 2]
                    last = pe.matmul(bank[:, (t % 2) * SEQ:(t % 2) * SEQ + VW], xT[:, t, :], row_w[:],
                                     start=True, stop=True)
                last.then_inc(rows_mm, 1)

            def key_products(n):
                wait(pe, xT_lo_ready, n + 1)
                wait(pe, xT_ready, n + 1)
                pe.matmul(ps_xk[:], g_hi[:], cols(xT_hi, n), start=True, stop=False)
                pe.matmul(ps_xk[:], g_hi[:], cols(xT_lo, n), start=False, stop=False)
                pe.matmul(ps_xk[:], g_lo[:], cols(xT_hi, n), start=False, stop=True).then_inc(key_mm, 1)

            def spread_index(n):
                wait(pe, rank_rows_ready, n + 1)
                wait(pe, route_ready, n)
                for t in range(NT):
                    last = pe.matmul(ps_route[:, t * P:(t + 1) * P], rank_rows[:, t, :], ident_bf[:],
                                     start=True, stop=True)
                last.then_inc(index_mm, 1)

            def transpose_route(n):
                wait(pe, onehot_ready, n + 1)
                wait(pe, index_ready, n + 1)
                for t in range(NT):
                    last = pe.transpose(ps_route[:, t * (P // 2):(t + 1) * (P // 2)].bitcast(BF16),
                                        onehot[:, t].rearrange("p q e -> p (q e)"), ident_bf[:])
                last.then_inc(route_mm, 1)

            def score_products(n):
                wait(pe, key_ready, n + 1)
                wait(pe, key_lo_ready, n + 1)
                wait(pe, route_rows_ready, 2 * n + 2)
                wait(pe, v_ready, 2 * n + 2)
                for s in range(NS):
                    xs_hi = xT_hi[:, bass.ds(n * GT + s * SEQ, SEQ)]
                    xs_lo = xT_lo[:, bass.ds(n * GT + s * SEQ, SEQ)]
                    acc = ps_a[:, s * SEQ:(s + 1) * SEQ]
                    pe.matmul(acc, keyT_hi[:, s, :], xs_hi, start=True, stop=False)
                    pe.matmul(acc, keyT_hi[:, s, :], xs_lo, start=False, stop=False)
                    pe.matmul(acc, keyT_lo[:, s, :], xs_hi, start=False, stop=True)
                for s in range(NS):
                    last = pe.matmul(ps_b[:, s * P:(s + 1) * P], keyT[:, 2 * s + 1, :], xT[:, 2 * s + 1, :],
                                     start=True, stop=True)
                last.then_inc(sc_mm, 1)

            def attention_products(n):
                wait(pe, sc_lo_ready, n + 1)
                wait(pe, v_lo_ready, n + 1)
                wait(pe, att_ready, n)
                for s in range(NS):
                    acc = ps_att[:, s * SEQ:(s + 1) * SEQ]
                    pe.matmul(acc, v_hi[:, s, :], sc0_hi[:, s, :], start=True, stop=False)
                    pe.matmul(acc, v_hi[:, s, :], sc0_lo[:, s, :], start=False, stop=False)
                    pe.matmul(acc, v_lo[:, s, :], sc0_hi[:, s, :], start=False, stop=False)
                    last = pe.matmul(ps_att[:, s * SEQ + P:(s + 1) * SEQ], v[:, 2 * s + 1, :], sc1[:, s, :],
                                     start=False, stop=True)
                last.then_inc(att_mm, 1)

            def keep_warm(count):
                for _ in range(count):
                    pe.matmul(ps_hid[0][:, 0:P], ones[:], ones[:], start=True, stop=True)

            pe.wait_ge(ones_ready, 1)
            keep_warm(WARM)
            pe.wait_ge(wattn_in, 16)
            wq, wk = wattn[:, A_Q:A_BQ], wattn[:, A_K:A_V]
            pe.matmul(ps_route[:, S_G:S_U], wk, wattn[:, A_Q:A_BK], start=True, stop=True)
            pe.matmul(ps_route[:, S_U:S_C], wq, wattn[:, A_BK:A_V], start=True, stop=True)
            pe.wait_ge(bqk_ready, 1)
            pe.matmul(ps_route[:, S_C:S_C + 1], ones[:], bqk[:], start=True, stop=True).then_inc(setup_mm, 1)
            pe.sem_inc(hid_used, RH)
            keep_warm(2)
            pe.wait_ge(const_in, 16)
            transpose_x(0)
            keep_warm(1)
            pe.wait_ge(roww_ready, 2)
            row_products(0)
            pe.wait_ge(g_lo_ready, 1)
            key_products(0)
            pe.wait_ge(w1_first_ready, 1)
            hidden(0, 0)
            hidden(0, 1)
            pe.wait_ge(ident_ready, 1)
            spread_index(0)
            pe.wait_ge(w1_lo_ready, 1)
            hidden(0, 2)
            hidden(0, 3)
            transpose_route(0)
            score_products(0)
            pe.wait_ge(b2_split, 5)
            pe.wait_ge(w2_first_ready, 1)
            pe.wait_ge(w2_lo_ready, 1)
            with pe.Fori(0, NG - 1) as g:
                n = g + 1
                hidden(g, 4)
                output(g, 0)
                hidden(g, 5)
                output(g, 1)
                hidden(g, 6)
                output_hi(g, 2)
                transpose_x(n)
                output_lo(g, 2)
                hidden(g, 7)
                row_products(n)
                attention_products(g)
                key_products(n)
                output(g, 3)
                hidden(n, 0)
                spread_index(n)
                output(g, 4)
                hidden(n, 1)
                output(g, 5)
                transpose_route(n)
                hidden(n, 2)
                output(g, 6)
                hidden(n, 3)
                output(g, 7)
                score_products(n)
            last = NG - 1
            hidden(last, 4)
            hidden(last, 5)
            last_output(0)
            hidden(last, 6)
            last_output(1)
            hidden(last, 7)
            last_output(2)
            last_output(3)
            attention_products(last)
            for b in range(LEAD, NB):
                last_output(b)


def kernel(L0_attn_x, L0_attn_W_qkv, L0_attn_b_qkv, L0_ffn_router_w, L0_ffn_router_b,
           L0_ffn_weights1, L0_ffn_bias1, L0_ffn_weights2, L0_ffn_bias2):
    import concourse.bacc as bacc
    from concourse.bass_utils import run_bass_kernel_spmd

    xs, w, b = np.asarray(L0_attn_x), np.asarray(L0_attn_W_qkv), np.asarray(L0_attn_b_qkv)
    b2 = np.asarray(L0_ffn_bias2)
    wq, wk, wv = w[0:D], w[D:2 * D], w[2 * D:]
    data = {
        "in_x": xs.reshape(TOK // P, P, D).transpose(1, 0, 2).reshape(P, TOK),
        "in_xT": xs.reshape(TOK, D).T,
        "in_wattn": np.concatenate([wq, b[0:D, None], b[D:2 * D, None], wk,
                                    wv.T, np.asarray(L0_ffn_router_w).T], axis=1),
        "in_bvr": np.concatenate([b[2 * D:], np.asarray(L0_ffn_router_b)]),
        "in_w1": np.asarray(L0_ffn_weights1).transpose(1, 0, 2).reshape(D, E * H),
        "in_w2": np.asarray(L0_ffn_weights2).reshape(NB, P, D).transpose(1, 0, 2).reshape(P, NB * D),
        "in_b1": np.asarray(L0_ffn_bias1).reshape(NB, P).T,
        "in_b2": np.concatenate([np.zeros_like(b2), b2, b2, b2]),
        "in_const": shape_constants(),
    }
    data = {k: np.ascontiguousarray(v) for k, v in data.items()}
    nc = bacc.Bacc("TRN2", target_bir_lowering=False, num_devices=1)
    aps = [nc.dram_tensor(k, v.shape, mybir.dt.from_np(v.dtype), kind="ExternalInput").ap()
           for k, v in data.items()]
    out = nc.dram_tensor("outT_d", (P, TOK), F32, kind="ExternalOutput").ap()
    build(nc, *aps, out)
    got = run_bass_kernel_spmd(nc, [data], core_ids=[0]).results[0]["outT_d"]
    return got.T.reshape(BATCH, SEQ, D)
```
